# Optimizing a Trainium2 kernel written in Bass

```python
import numpy as np
import jax
import jax.numpy as jnp

def _softmax(x, axis=-1):
    return jax.nn.softmax(x, axis=axis)

def _gelu(x):
    return jax.nn.gelu(x, approximate=True)

def _silu(x):
    return jax.nn.silu(x)

def _sigmoid(x):
    return jax.nn.sigmoid(x)

def _layernorm(x, axis=-1, eps=1e-05):
    m = jnp.mean(x, axis=axis, keepdims=True)
    v = jnp.var(x, axis=axis, keepdims=True)
    return (x - m) / jnp.sqrt(v + eps)

def _scatter_add(tgt, idx, src, axis=0):
    return tgt.at[idx].add(src)

def _segment_sum(src, seg, n):
    return jax.ops.segment_sum(src, seg, n)
kernel_name = 'mk_gnn_preln_d4_gnn_r8_b3ed9d'

def setup_inputs(seed: int=0):
    np.random.seed(seed)
    _w = jnp.asarray

    def _rec_inputs():
        import jax
        import jax.numpy as jnp
        _gk = jax.random.key(seed)
        x = -0.000202 + 1 * jax.random.normal(jax.random.fold_in(_gk, 1), (6250, 128), jnp.float32)
        _s = jax.random.randint(jax.random.fold_in(_gk, 2), (50000,), 0, 6250, jnp.int32)
        _d = jax.random.randint(jax.random.fold_in(_gk, 3), (50000,), 0, 6250, jnp.int32)
        _loop = jnp.arange(6250, dtype=jnp.int32)
        src = jnp.concatenate([_s, _d, _loop])
        dst = jnp.concatenate([_d, _s, _loop])
        _o = jnp.argsort(dst, stable=True)
        src = src[_o]
        dst = dst[_o]
        edge_attr3_1x20 = jax.random.uniform(jax.random.fold_in(_gk, 12), (106250, 1, 20), jnp.float32, 0.0, 1)
        edge_weight = jax.random.uniform(jax.random.fold_in(_gk, 14), (106250,), jnp.float32, 0.0, 0.999998)
        edge_weight1 = jax.random.uniform(jax.random.fold_in(_gk, 15), (106250, 1), jnp.float32, 0.0, 0.999999)
        return (x, src, dst, edge_attr3_1x20, edge_weight, edge_weight1)
    x, src, dst, edge_attr3_1x20, edge_weight, edge_weight1 = _rec_inputs()

    def _L0_gnn_setup():
        import jax, jax.numpy as jnp
        import numpy as np
        N_ATOMS = 6250
        N_PAIRS = 75000
        D_FEAT = 128
        D_FILT = 128
        N_RBF = 20

        def ssp(x):
            return jax.nn.softplus(x) - jnp.log(2.0).astype(x.dtype)
        key = jax.random.key(seed)
        ks = jax.random.split(key, 12)
        inp = {'x': jax.random.normal(ks[0], (N_ATOMS, D_FEAT), dtype=jnp.float32), 'pairlist': jax.random.randint(ks[1], (2, N_PAIRS), 0, N_ATOMS, dtype=jnp.int64), 'f_ij': jax.random.uniform(ks[2], (N_PAIRS, 1, N_RBF), dtype=jnp.float32), 'f_ij_cutoff': jax.random.uniform(ks[3], (N_PAIRS, 1), dtype=jnp.float32), 'W_in': jax.random.normal(ks[4], (D_FEAT, D_FILT), dtype=jnp.float32) * 0.05, 'W_f1': jax.random.normal(ks[5], (N_RBF, D_FILT), dtype=jnp.float32) * 0.05, 'b_f1': jnp.zeros((D_FILT,), dtype=jnp.float32), 'W_f2': jax.random.normal(ks[6], (D_FILT, D_FILT), dtype=jnp.float32) * 0.05, 'b_f2': jnp.zeros((D_FILT,), dtype=jnp.float32), 'W_o1': jax.random.normal(ks[7], (D_FILT, D_FEAT), dtype=jnp.float32) * 0.05, 'b_o1': jnp.zeros((D_FEAT,), dtype=jnp.float32), 'W_o2': jax.random.normal(ks[8], (D_FEAT, D_FEAT), dtype=jnp.float32) * 0.05, 'b_o2': jnp.zeros((D_FEAT,), dtype=jnp.float32)}
        return inp
    _L0_gnn_all = _L0_gnn_setup()
    _L0_gnn_in = {k: v for k, v in _L0_gnn_all.items() if k in ('W_in', 'W_f1', 'b_f1', 'W_f2', 'b_f2', 'W_o1', 'b_o1', 'W_o2', 'b_o2')}
    del _L0_gnn_all

    def _L1_gnn_setup():
        import jax, jax.numpy as jnp
        import numpy as np
        N_NODES = 6250
        N_EDGES = 100000
        IN_DIM = 128
        OUT_DIM = 128
        NEG_SLOPE = 0.01
        key = jax.random.key(seed)
        k_h, k_src, k_dst, k_w, k_as, k_ad = jax.random.split(key, 6)
        h = jax.random.normal(k_h, (N_NODES, IN_DIM), dtype=jnp.float32)
        src = jax.random.randint(k_src, (N_EDGES,), 0, N_NODES, dtype=jnp.int32)
        dst = jax.random.randint(k_dst, (N_EDGES,), 0, N_NODES, dtype=jnp.int32)
        gain = float(np.sqrt(2.0))
        std_w = gain * np.sqrt(2.0 / (IN_DIM + OUT_DIM))
        W = jax.random.normal(k_w, (IN_DIM, OUT_DIM), dtype=jnp.float32) * std_w
        std_a = gain * np.sqrt(2.0 / (2 * OUT_DIM + 1))
        a_src = jax.random.normal(k_as, (OUT_DIM,), dtype=jnp.float32) * std_a
        a_dst = jax.random.normal(k_ad, (OUT_DIM,), dtype=jnp.float32) * std_a
        return {'h': h, 'src': src, 'dst': dst, 'W': W, 'a_src': a_src, 'a_dst': a_dst}
    _L1_gnn_all = _L1_gnn_setup()
    _L1_gnn_in = {k: v for k, v in _L1_gnn_all.items() if k in ('W', 'a_src', 'a_dst')}
    del _L1_gnn_all

    def _L2_gnn_setup():
        import jax, jax.numpy as jnp
        import numpy as np
        N_NODES = 12500
        N_EDGES = 200000
        IN_FEATS = 128
        N_HIDDEN = 128
        key = jax.random.key(seed)
        k1, k2, k3, k4 = jax.random.split(key, 4)
        features = jax.random.normal(k1, (N_NODES, IN_FEATS), dtype=jnp.float32)
        src = jax.random.randint(k2, (N_EDGES,), 0, N_NODES, dtype=jnp.int32)
        dst = jax.random.randint(k3, (N_EDGES,), 0, N_NODES, dtype=jnp.int32)
        weight = jax.random.normal(k4, (IN_FEATS, N_HIDDEN), dtype=jnp.float32) * (1.0 / np.sqrt(IN_FEATS))
        bias = jnp.zeros((N_HIDDEN,), dtype=jnp.float32)
        return {'features': features, 'src': src, 'dst': dst, 'weight': weight, 'bias': bias}
    _L2_gnn_all = _L2_gnn_setup()
    _L2_gnn_in = {k: v for k, v in _L2_gnn_all.items() if k in ('weight', 'bias')}
    del _L2_gnn_all

    def _L3_gnn_setup():
        import jax, jax.numpy as jnp
        import numpy as np
        N_NODES = 6250
        NM_SCALE = 3

        def gcn_conv(x, src, dst, ew, W, b, n):
            h = x @ W
            deg = jax.ops.segment_sum(ew, dst, num_segments=n)
            dinv = jnp.where(deg > 0, jax.lax.rsqrt(deg), 0.0)
            norm = dinv[src] * ew * dinv[dst]
            out = jax.ops.segment_sum(h[src] * norm[:, None], dst, num_segments=n)
            return out + b

        def prelu(z, slope):
            return jnp.where(z >= 0, z, slope * z)
        key = jax.random.key(seed)
        ks = jax.random.split(key, 8)
        d_in, d_h = (128, 128)
        E = 100000
        x = jax.random.normal(ks[0], (N_NODES, d_in), dtype=jnp.float32)
        edge_index = jax.random.randint(ks[1], (2, E), 0, N_NODES, dtype=jnp.int64)
        edge_weight = jax.random.uniform(ks[2], (E,), dtype=jnp.float32)
        W0 = jax.random.normal(ks[3], (d_in, d_h), dtype=jnp.float32) / np.sqrt(d_in)
        b0 = jnp.zeros((d_h,), dtype=jnp.float32)
        W1 = jax.random.normal(ks[4], (d_h, d_h), dtype=jnp.float32) / np.sqrt(d_h)
        b1 = jnp.zeros((d_h,), dtype=jnp.float32)
        prelu_w = jnp.full((d_h,), 0.25, dtype=jnp.float32)
        mixing = jnp.full((NM_SCALE, 1), 1.0 / NM_SCALE, dtype=jnp.float32)
        return {'x': x, 'edge_index': edge_index, 'edge_weight': edge_weight, 'W0': W0, 'b0': b0, 'W1': W1, 'b1': b1, 'prelu_w': prelu_w, 'mixing': mixing}
    _L3_gnn_all = _L3_gnn_setup()
    _L3_gnn_in = {k: v for k, v in _L3_gnn_all.items() if k in ('W0', 'b0', 'W1', 'b1', 'prelu_w', 'mixing')}
    del _L3_gnn_all
    return {'x': x, 'src': src, 'dst': dst, 'edge_attr3_1x20': edge_attr3_1x20, 'edge_weight': edge_weight, 'edge_weight1': edge_weight1, 'L0_gnn_W_in': _L0_gnn_in['W_in'], 'L0_gnn_W_f1': _L0_gnn_in['W_f1'], 'L0_gnn_b_f1': _L0_gnn_in['b_f1'], 'L0_gnn_W_f2': _L0_gnn_in['W_f2'], 'L0_gnn_b_f2': _L0_gnn_in['b_f2'], 'L0_gnn_W_o1': _L0_gnn_in['W_o1'], 'L0_gnn_b_o1': _L0_gnn_in['b_o1'], 'L0_gnn_W_o2': _L0_gnn_in['W_o2'], 'L0_gnn_b_o2': _L0_gnn_in['b_o2'], 'L1_gnn_W': _L1_gnn_in['W'], 'L1_gnn_a_src': _L1_gnn_in['a_src'], 'L1_gnn_a_dst': _L1_gnn_in['a_dst'], 'L2_gnn_weight': _L2_gnn_in['weight'], 'L2_gnn_bias': _L2_gnn_in['bias'], 'L3_gnn_W0': _L3_gnn_in['W0'], 'L3_gnn_b0': _L3_gnn_in['b0'], 'L3_gnn_W1': _L3_gnn_in['W1'], 'L3_gnn_b1': _L3_gnn_in['b1'], 'L3_gnn_prelu_w': _L3_gnn_in['prelu_w'], 'L3_gnn_mixing': _L3_gnn_in['mixing']}

def reference(x, src, dst, edge_attr3_1x20, edge_weight, edge_weight1, L0_gnn_W_in, L0_gnn_W_f1, L0_gnn_b_f1, L0_gnn_W_f2, L0_gnn_b_f2, L0_gnn_W_o1, L0_gnn_b_o1, L0_gnn_W_o2, L0_gnn_b_o2, L1_gnn_W, L1_gnn_a_src, L1_gnn_a_dst, L2_gnn_weight, L2_gnn_bias, L3_gnn_W0, L3_gnn_b0, L3_gnn_W1, L3_gnn_b1, L3_gnn_prelu_w, L3_gnn_mixing):
    import jax
    import jax.numpy as jnp

    def _L0_gnn_ref(x, pairlist, f_ij, f_ij_cutoff, W_in, W_f1, b_f1, W_f2, b_f2, W_o1, b_o1, W_o2, b_o2):
        import jax, jax.numpy as jnp
        import numpy as np
        N_ATOMS = 6250
        N_PAIRS = 75000
        D_FEAT = 128
        D_FILT = 128
        N_RBF = 20

        def ssp(x):
            return jax.nn.softplus(x) - jnp.log(2.0).astype(x.dtype)
        n_atoms = x.shape[0]
        h = x @ W_in
        Wij = ssp(f_ij[:, 0, :] @ W_f1 + b_f1) @ W_f2 + b_f2
        idx_i = pairlist[0]
        idx_j = pairlist[1]
        x_ij = h[idx_j] * Wij * f_ij_cutoff
        agg = jax.ops.segment_sum(x_ij, idx_i, num_segments=n_atoms)
        out = ssp(agg @ W_o1 + b_o1) @ W_o2 + b_o2
        return out

    def _L1_gnn_ref(h, src, dst, W, a_src, a_dst):
        import jax, jax.numpy as jnp
        import numpy as np
        N_NODES = 6250
        N_EDGES = 100000
        IN_DIM = 128
        OUT_DIM = 128
        NEG_SLOPE = 0.01
        n = h.shape[0]
        z = h @ W
        e = z[src] @ a_src + z[dst] @ a_dst
        e = jnp.where(e >= 0, e, NEG_SLOPE * e)
        m = jax.ops.segment_max(e, dst, num_segments=n)
        m = jnp.where(jnp.isfinite(m), m, 0.0)
        ex = jnp.exp(e - m[dst])
        denom = jax.ops.segment_sum(ex, dst, num_segments=n)
        denom = jnp.where(denom > 0, denom, 1.0)
        alpha = ex / denom[dst]
        out = jax.ops.segment_sum(alpha[:, None] * z[src], dst, num_segments=n)
        return out

    def _L2_gnn_ref(features, src, dst, weight, bias):
        import jax, jax.numpy as jnp
        import numpy as np
        N_NODES = 12500
        N_EDGES = 200000
        IN_FEATS = 128
        N_HIDDEN = 128
        "DGL GraphConv with norm='both' + relu activation.\n            out = relu( D_dst^{-1/2} * segment_sum( (D_src^{-1/2} x)[src] -> dst ) @ W + b )\n            "
        n = features.shape[0]
        ones_e = jnp.ones(src.shape[0], dtype=features.dtype)
        deg_out = jnp.clip(jax.ops.segment_sum(ones_e, src, num_segments=n), 1.0)
        deg_in = jnp.clip(jax.ops.segment_sum(ones_e, dst, num_segments=n), 1.0)
        h = features * jax.lax.rsqrt(deg_out)[:, None]
        agg = jax.ops.segment_sum(h[src], dst, num_segments=n)
        agg = agg * jax.lax.rsqrt(deg_in)[:, None]
        out = agg @ weight + bias
        return jax.nn.relu(out)

    def _L3_gnn_ref(x, edge_index, edge_weight, W0, b0, W1, b1, prelu_w, mixing):
        import jax, jax.numpy as jnp
        import numpy as np
        N_NODES = 6250
        NM_SCALE = 3

        def gcn_conv(x, src, dst, ew, W, b, n):
            h = x @ W
            deg = jax.ops.segment_sum(ew, dst, num_segments=n)
            dinv = jnp.where(deg > 0, jax.lax.rsqrt(deg), 0.0)
            norm = dinv[src] * ew * dinv[dst]
            out = jax.ops.segment_sum(h[src] * norm[:, None], dst, num_segments=n)
            return out + b

        def prelu(z, slope):
            return jnp.where(z >= 0, z, slope * z)
        n = x.shape[0]
        loop = jnp.arange(n, dtype=edge_index.dtype)
        src = jnp.concatenate([edge_index[0], loop])
        dst = jnp.concatenate([edge_index[1], loop])
        ew = jnp.concatenate([edge_weight, jnp.ones((n,), dtype=edge_weight.dtype)])

        def features(z):
            z = prelu(gcn_conv(z, src, dst, ew, W0, b0, n), prelu_w)
            z = prelu(gcn_conv(z, src, dst, ew, W1, b1, n), prelu_w)
            return z
        feats_T = jnp.stack([features(x) for _ in range(NM_SCALE)])
        coeff = jax.nn.softmax(mixing, axis=0).squeeze(-1)
        return jnp.einsum('tnj,t->nj', feats_T, coeff)
    edge_index = jnp.stack([src, dst])
    h = jnp.maximum(_layernorm(x, axis=-1), 0.0)
    x = x + _L0_gnn_ref(h, edge_index, edge_attr3_1x20, edge_weight1, L0_gnn_W_in, L0_gnn_W_f1, L0_gnn_b_f1, L0_gnn_W_f2, L0_gnn_b_f2, L0_gnn_W_o1, L0_gnn_b_o1, L0_gnn_W_o2, L0_gnn_b_o2)
    h = jnp.maximum(_layernorm(x, axis=-1), 0.0)
    x = x + _L1_gnn_ref(h, src, dst, L1_gnn_W, L1_gnn_a_src, L1_gnn_a_dst)
    h = jnp.maximum(_layernorm(x, axis=-1), 0.0)
    x = x + _L2_gnn_ref(h, src, dst, L2_gnn_weight, L2_gnn_bias)
    h = jnp.maximum(_layernorm(x, axis=-1), 0.0)
    x = x + _L3_gnn_ref(h, edge_index, edge_weight, L3_gnn_W0, L3_gnn_b0, L3_gnn_W1, L3_gnn_b1, L3_gnn_prelu_w, L3_gnn_mixing)
    return x

_drawn_inputs = setup_inputs


def setup_inputs(seed=0):
    import zlib

    import numpy as np

    out = dict(_drawn_inputs(seed))
    spreads = {'L0_gnn_b_f1': (0.0, 0.8),
     'L0_gnn_b_f2': (0.0, 0.376),
     'L0_gnn_b_o1': (0.0, 2.0),
     'L0_gnn_b_o2': (0.0, 0.8),
     'L2_gnn_bias': (0.0, 0.8),
     'L3_gnn_b0': (0.0, 0.8),
     'L3_gnn_b1': (0.0, 0.8),
     'L3_gnn_prelu_w': (0.25, 0.6),
     'L3_gnn_mixing': (0.3333333432674408, 0.6)}
    factors = {'edge_attr3_1x20': 8.0,
     'edge_weight': 101.779,
     'edge_weight1': 7.336,
     'L0_gnn_W_f1': 3.969,
     'L0_gnn_W_f2': 3.333,
     'L1_gnn_a_src': 25.388,
     'L1_gnn_a_dst': 37.439,
     'L3_gnn_W0': 2.866,
     'L3_gnn_W1': 2.917}
    for name, (base, spread) in spreads.items():
        noise = np.random.default_rng([zlib.crc32(name.encode()), seed]).standard_normal(out[name].shape)
        drawn = base * np.exp(spread * noise) if base else spread * noise
        out[name] = jnp.asarray(drawn.astype(out[name].dtype))
    for name, factor in factors.items():
        out[name] = (out[name] * factor).astype(out[name].dtype)
    return out
```

```python
from contextlib import ExitStack

import numpy as np

import concourse.bass as bass
from concourse import mybir

F32 = mybir.dt.float32
BF16 = mybir.dt.bfloat16
I32 = mybir.dt.int32
ALU = mybir.AluOpType
ACT = mybir.ActivationFunctionType
AX = mybir.AxisListType

P = 128
D = 128
TILES = 8
CHUNK = P * TILES
ROWS = 4
SUMS = 4
NODES_PER_BATCH = 7
EPS = 1e-5
NO_NODE = -1
SLOPE_GAT = 0.01


class Place:

    def __init__(self, i, n, blocks, w=None, general=False):
        self.c = i * ROWS + n
        self.r, self.turn = n % ROWS, i + n // ROWS
        self.k, self.turn2 = n % 2, i * 2 + n // 2
        self.w, self.general = w, general
        self.s = self.c if w is None else self.c * blocks + w
        self.cols = bass.ds(self.c * TILES, TILES)


class Counter:

    def __init__(self, sem, base):
        self.sem, self.base = sem, base


def build_program(nc, a, out):
    N, _ = a["x"].shape
    E_COLS = a["src"].shape[1]
    CHUNKS = E_COLS // TILES
    BLOCKS = -(-N // P)
    FULL = N // P
    REST = N - FULL * P
    NPAD = BLOCKS * P
    RBF = a["attr"].shape[0]
    NJ = BLOCKS // NODES_PER_BATCH
    BJ = NODES_PER_BATCH
    BW = BJ * P
    HALF = BW // 2
    TW = D + 4
    ONE, ZS, ZD = D, D + 1, D + 2
    ACC = NPAD + P
    MIX = a["mixing"].shape[1]
    assert BLOCKS % BJ == 0 and CHUNKS % ROWS == 0

    tables = [nc.dram_tensor(f"table_{n}", [NPAD if n > 1 else ACC, TW if n == 1 else D], F32, kind="Internal").ap()
              for n in range(5)]
    sums_dram = [nc.dram_tensor(f"sums_{q}", [ACC, D], F32, kind="Internal").ap() for q in range(SUMS)]

    with ExitStack() as ctx:
        def sb(name, cols, dt=F32, rows=P):
            return ctx.enter_context(nc.sbuf_tensor(name, [rows, cols], dt))

        def pb(name, cols, dt=F32):
            return ctx.enter_context(nc.psum_tensor(name, [P, cols], dt))

        def sem(name):
            return ctx.enter_context(nc.semaphore(name))

        def sems(prefix, names):
            return {n: sem(f"{prefix}_{n}") for n in names.split()}

        X = sb("X", BLOCKS * D)
        acc = sb("acc", ACC)
        top = sb("top", max(ACC, 6 * CHUNK))
        stage = sb("stage", max(BLOCKS * TW, ACC, 3 * CHUNK))
        den = stage[:, 0:ACC]
        G = [sb(f"G{r}", TILES * TW) for r in range(ROWS)]
        idx = [sb(f"idx{r}", TILES, I32) for r in range(ROWS)]
        dst_i = sb("dst_i", E_COLS, I32)
        dst = sb("dst", E_COLS)
        ew = sb("ew", E_COLS)
        cut = sb("cut", E_COLS)
        srcf = sb("srcf", E_COLS)
        srch = sb("srch", E_COLS)
        srcl = sb("srcl", E_COLS)
        S = [sb(f"S{k}", CHUNK) for k in range(2)]
        big = [sb(f"big{k}", CHUNK) for k in range(5)]
        dloc = [sb(f"dloc{k}", TILES) for k in range(2)]
        ident = sb("ident", P)
        iota = sb("iota", P)
        ones = sb("ones", P)
        iota_i = sb("iota_i", P, I32)
        first = sb("first", CHUNKS)
        wbase = sb("wbase", BLOCKS)
        flag_i = sb("flag_i", 1, I32)
        W = {n: sb(f"w_{n}", D) for n in ("in", "f2", "o1", "o2", "gat", "gc", "g0", "g1")}
        wf1 = sb("wf1", D, rows=RBF)
        attr = [sb(f"attr{k}", CHUNK, rows=RBF) for k in range(2)]
        bf1 = sb("bf1", 1)
        bo1 = sb("bo1", 1)
        rowb = {n: sb(f"row_{n}", D) for n in ("bf2", "bo2", "asrc", "adst", "gc", "b0", "b1", "slope")}
        vsrc = sb("vsrc", D)
        vdst = sb("vdst", D)
        vcol = sb("vcol", 2)
        mix = sb("mix", 8)
        csum = sb("csum", 1)
        stat = sb("stat", BLOCKS * 6)
        col = {n: sb(f"col_{n}", BLOCKS) for n in
               ("mean", "diff", "var", "std", "rstd", "scale", "bias", "dout", "din", "dinv", "t0", "t1", "zs", "zd")}
        hist = sb("hist", BLOCKS)
        degrow = top[0:2, :]
        small = {n: [sb(f"sm_{n}{k}", TILES) for k in range(2)] for n in ("zde", "l", "b", "ex")}
        mcol = {n: [sb(f"mc_{n}{k}", 2) for k in range(2)] for n in ("mx", "old", "t", "l", "pair", "zd")}
        tmp = [sb(f"tmp{k}", P) for k in range(6)]
        onesew = [sb(f"onesew{k}", TILES * 2) for k in range(2)]
        viol = sb("viol", 4)
        gmin = sb("gmin", 4)
        half = sb("half", 1)
        msg = [top[:, k * CHUNK:(k + 1) * CHUNK] for k in range(2)]
        nm_sb = sb("nm_sb", D + 4)
        top_old = sb("top_old", P)
        top_diag = sb("top_diag", P)
        decay = [sb(f"decay{k}", P) for k in range(2)]
        w7 = msg[0][:, 0:BW]
        src_row = [top[:, (2 + k) * CHUNK:(3 + k) * CHUNK].bitcast(I32) for k in range(2)]
        dst_row = [top[:, (4 + k) * CHUNK:(5 + k) * CHUNK].bitcast(I32) for k in range(2)]
        same = [stage[:, k * CHUNK:(k + 1) * CHUNK] for k in range(2)]
        earlier = stage[:, 2 * CHUNK:3 * CHUNK]
        src_i = stage[:, 0:E_COLS].bitcast(I32)
        h_win = [sb(f"h_win{k}", D) for k in range(2)]
        node_id = [sb(f"node_id{k}", 1) for k in range(2)]
        gather_idx = sb("gather_idx", TILES, I32)
        gather_f = sb("gather_f", TILES)
        dup = {n: sb(f"dup_{n}", TILES) for n in ("count", "is", "away", "to")}
        tri = sb("tri", P)
        pidx = sb("pidx", 1)
        pidx_i = sb("pidx_i", 1, I32)
        trash = sb("trash", 1)
        bf2_part = [sb(f"bf2_part{k}", D, BF16) for k in range(3)]
        bf2_rows = sb("bf2_rows", D, BF16)
        ones16 = sb("ones16", P, BF16)
        far = [big[q][:, 0:E_COLS] for q in range(4)]
        big_i = big[0][:, 0:E_COLS].bitcast(I32)
        score = sb("score", 2 * BJ)
        deg = sb("deg", 2 * BLOCKS)
        degroot = sb("degroot", 2 * BLOCKS)
        dinv = sb("dinv", 2 * BLOCKS)
        positive = sb("positive", BLOCKS)
        lohot = sb("lohot", TILES * P, BF16)
        hihot = sb("hihot", TILES * BLOCKS, BF16)
        h7 = big[0][:, 0:BW]
        lhs7 = big[1][:, 0:BW]
        t7 = big[2][:, 0:BW]
        u7 = big[3][:, 0:BW]
        v7 = big[4][:, 0:BW]

        psA = pb("psA", 1024)
        psB = pb("psB", 1024)
        psC = pb("psC", 512)
        psD = pb("psD", 512)
        psE = pb("psE", 512)
        psF = pb("psF", 512)

        loaded = sem("loaded")
        pool_consts = sem("pool_consts")
        dve_link = sem("dve_link")
        x_tail = sem("x_tail")
        pro = sems("pro", "dst first_row vdiag vrow mix_max mix_exp viol viol_all flag gmin gmin_all scores")
        turns = sem("turns")
        idx_in = [sem(f"idx_in{r}") for r in range(ROWS)]
        rows_in = [sem(f"rows_in{r}") for r in range(ROWS)]
        zd_in = [sem(f"zd_in{k}") for k in range(2)]
        table_out = sem("table_out")
        begun = sem("begun")
        acc_ready = sem("acc_ready")
        out_done = sem("out_done")
        norm = "bn stats1 std1 cols1"
        phases = (
            f"{norm} h tr lhs prod rows",
            f"tr turned mm abs relu exp ln lhs prod upd resid {norm} h scored kept rows",
            f"deg1 root1 lhs prod upd {norm} rows",
            f"counts1 deg1 root1 lhs prod upd biased resid {norm} h tr turned rows",
            "lhs prod upd biased neg prelu h tr turned rows",
            "lhs prod upd biased neg prelu resid")
        node_sems = {name: sem(f"node_{name}") for name in sorted({m.strip("1") for p in phases for m in p.split()})}
        nd, counted = [], dict.fromkeys(node_sems, 0)
        for phase in phases:
            names = {m.strip("1"): 1 if m.endswith("1") else NJ for m in phase.split()}
            nd.append({m: Counter(node_sems[m], counted[m]) for m in names})
            for m, n in names.items():
                counted[m] += n
        l0 = sems("l0", "pre abs relu exp ln ssp wij node_id spread rows rows_low rows_high msg same compared counted "
                        "dup away moved to idx summed out_low out gidx_f gidx gathered over")
        rows_at = [sem(f"rows_at{k}") for k in range(2)]
        h_in = [sem(f"h_in{k}") for k in range(2)]
        zeroed = sem("zeroed")
        sums_clear = sem("sums_clear")
        summed = [sem(f"summed{q}") for q in range(SUMS)]
        all_summed = sem("all_summed")
        sums_in = sem("sums_in")
        l1 = sems("l1", "hot hist counted dloc onehot diag masked mx st old_row old_col t1 t2 pair top_diag edge toprow zde leak arg0 "
                        "arg decay_arg top_new ex decay weights nm nm_sb tr scaled added")
        lw = {n: sems(f"l{n}", "dloc onehot sums added" + (" ones" if n == 2 else "")) for n in (2, 3, 4)}

        links = Counter(dve_link, 0)
        TABLE_DMAS = [NJ + 1, NJ + 3, 2 * NJ + 3, 3 * NJ + 3, 4 * NJ + 3]
        TURNS = CHUNKS // ROWS

        LOADS = [(t[:, :], what) for t, what in (
            (dst_i, a["dst"]), (src_i, a["src"]), (ew, a["ew"]), (cut, a["cut"]), (W["in"], a["w_in"]), (W["f2"], a["w_f2"]),
            (W["o1"], a["w_o1"]), (W["o2"], a["w_o2"]), (W["gat"], a["w_gat"]), (W["gc"], a["w_gc"]), (W["g0"], a["w_0"]),
            (W["g1"], a["w_1"]), (wf1, a["w_f1"]), (bf1, a["b_f1"]), (bo1, a["b_o1"]))]
        LOADS += [(rowb[n][:, :], what.to_broadcast([P, D])) for n, what in (
            ("bf2", a["b_f2"]), ("bo2", a["b_o2"]), ("asrc", a["a_src"]), ("adst", a["a_dst"]), ("gc", a["b_gc"]), ("b0", a["b_0"]),
            ("b1", a["b_1"]), ("slope", a["slope"]))]
        LOADS += [(mix[:, 0:MIX], a["mixing"].to_broadcast([P, MIX]))]

        def link(ins):
            links.base += 1
            ins.then_inc(dve_link, 1)
            nc.vector.wait_ge(dve_link, links.base)

        def walk(eng, general, over, near, every_chunk, every_step, lags, credit=False,
                 steps=BLOCKS):
            with eng.If(general > 0):
                if credit:
                    eng.sem_inc(over, 1)
                with eng.Fori(0, CHUNKS // ROWS) as i:
                    for r in range(ROWS):
                        st = Place(i, r, BLOCKS, general=True)
                        if every_chunk:
                            eng.wait_ge(over, st.c * steps + 1)
                            if eng is nc.gpsimd:
                                eng.sem_inc(turns, 1)
                            for stage_ in every_chunk:
                                stage_(st)
                        if every_step:
                            with eng.Fori(0, BLOCKS) as w:
                                st = Place(i, r, BLOCKS, w, general=True)
                                eng.wait_ge(over, st.s + 1)
                                for stage_ in every_step:
                                    stage_(st)
                if credit:
                    eng.wait_ge(over, CHUNKS * steps + 1)
            with eng.Else():
                def turn(i, n):
                    for stage_, lag in near:
                        if not isinstance(i, int) or 0 <= n - lag < CHUNKS:
                            stage_(Place(i, n - lag, BLOCKS))
                for n in range(ROWS):
                    turn(0, n)
                with eng.Fori(0, CHUNKS // ROWS - 1) as i:
                    for n in range(ROWS, 2 * ROWS):
                        turn(i, n)
                for n in range(CHUNKS, CHUNKS + lags):
                    turn(0, n)
                if credit and steps > 1:
                    eng.wait_ge(over, CHUNKS)

        def ready(eng, semaphore, st):
            eng.wait_ge(semaphore, st.s + 1)

        def done_before(eng, semaphore, st, depth):
            if not st.general and not (isinstance(st.s, int) and st.s < depth):
                eng.wait_ge(semaphore, st.s + (1 - depth))

        def batches(eng, body):
            body(0)
            with eng.Fori(1, NJ) as j:
                body(j)

        def reached(eng, counter, n):
            eng.wait_ge(counter.sem, n + counter.base)

        def batch_before(eng, counter, j):
            if not (isinstance(j, int) and j == 0):
                reached(eng, counter, j)

        def tiles(ap, n=TILES):
            return ap.rearrange("p (t f) -> p t f", t=n)

        def over_tiles(ap):
            return ap.unsqueeze(1).to_broadcast([P, TILES, ap.shape[1]])

        def over_blocks(ap):
            return ap.unsqueeze(1).to_broadcast([P, BJ, ap.shape[1]])

        def along(ap, n):
            return ap.unsqueeze(2).to_broadcast([P, ap.shape[1], n])

        def slot(st):
            return st.k if st.w is None else 0

        def hot(st):
            return (S[0], S[1], big[3], big[4])[st.r if st.w is None else 0]

        def bank(st):
            return (psD, psE)[slot(st)]

        def indices_ready(eng, n, st):
            eng.wait_ge(idx_in[st.r], 16 * (st.turn + ((n - 1) * TURNS + 1)))

        def rows_ready(eng, n, st):
            eng.wait_ge(rows_in[st.r], 16 * TILES * (st.turn + ((n - 1) * TURNS + 1)))

        def window(eng, st):
            if st.w is not None:
                return st.w * P
            return eng.value_load(dst_i[0:1, bass.ds(st.c * TILES, 1)], min_val=0, max_val=N - 1)

        def batch(j, width=D):
            return bass.ds(j * (BJ * width), BJ * width)

        block = ctx.enter_context(nc.Block())

        @block.sync
        def _(sp):
            sp.dma_start(tiles(X[:, 0:FULL * D], FULL),
                         a["x"][0:FULL * P, :].rearrange("(b p) f -> p b f", p=P)).then_inc(loaded, 16)
            if REST:
                sp.wait_ge(x_tail, 1)
                sp.dma_start(X[0:REST, FULL * D:BLOCKS * D], a["x"][FULL * P:N, :]).then_inc(loaded, 16)
            for to, what in LOADS:
                sp.dma_start(to, what).then_inc(loaded, 16)

            sp.wait_ge(pro["flag"], 1)
            general = sp.value_load(flag_i[0:1, 0:1], min_val=0, max_val=1)

            def write_table(n):
                def one(j):
                    reached(sp, nd[n]["rows"], j + 1)
                    sp.dma_start(tables[n][bass.ds(j * BW, BW), :].rearrange("(b p) f -> p b f", p=P),
                                 tiles(stage[:, batch(j)], BJ)).then_inc(table_out, 16)
                with sp.Fori(0, NJ) as j:
                    one(j)

            def load_indices(n):
                def stage_(st):
                    if not (isinstance(st.turn, int) and st.turn == 0 and n == 1) and not st.general:
                        sp.wait_ge(rows_in[st.r], 16 * TILES * (st.turn + (n - 1) * TURNS))
                    sp.dma_start(idx[st.r][:, :], a["src"][:, st.cols]).then_inc(idx_in[st.r], 16)
                return stage_

            def load_edges(st):
                done_before(sp, l0["to"], st, 2)
                done_before(sp, l0["spread"], st, 2)
                done_before(sp, l0["pre"], st, 2)
                sp.dma_start(src_row[st.k], a["src_row"][:, bass.ds(st.c * CHUNK, CHUNK)]
                             .to_broadcast([P, CHUNK])).then_inc(rows_at[st.k], 16)
                sp.dma_start(attr[st.k][:, :], a["attr"][:, bass.ds(st.c * CHUNK, CHUNK)]).then_inc(rows_at[st.k], 16)
                sp.dma_start(dst_row[st.k], a["dst_row"][:, bass.ds(st.c * CHUNK, CHUNK)]
                             .to_broadcast([P, CHUNK])).then_inc(rows_at[st.k], 16)

            def load_window(st):
                done_before(sp, l0["rows"], st, 2)
                sp.sem_inc(turns, 1)
                sp.dma_start(h_win[st.k][:, :], tables[0][bass.ds(window(sp, st), P), :]).then_inc(h_in[st.k], 16)

            def load_zd(st):
                done_before(sp, l1["pair"], st, 2)
                sp.sem_inc(turns, 1)
                k = 0 if st.w is not None else st.k
                sp.dma_start(mcol["zd"][k][:, 0:2], tables[1][bass.ds(window(sp, st), P), ZD:ZD + 2]).then_inc(zd_in[k], 16)

            for q in range(SUMS):
                sp.wait_ge(zeroed, 1)
                sp.dma_start(sums_dram[q].rearrange("(p n) f -> p (n f)", p=P), acc[:, 0:ACC]).then_inc(sums_clear, 16)
            write_table(0)
            sp.dma_start(tables[0][NPAD:ACC, :], stage[:, 0:D]).then_inc(table_out, 16)
            sp.wait_ge(table_out, 16 * TABLE_DMAS[0])
            walk(sp, general, l0["over"], [(load_edges, 0), (load_window, 0)], [load_edges], [], 0, steps=1)
            sp.wait_ge(all_summed, 1)

            def load_sums(j):
                batch_before(sp, nd[1]["tr"], j)
                for q in range(SUMS):
                    sp.dma_start(tiles(G[q][:, 0:BW], BJ), sums_dram[q][bass.ds(j * BW, BW), :]
                                 .rearrange("(b p) f -> p b f", p=P)).then_inc(sums_in, 16)
            batches(sp, load_sums)
            sp.wait_ge(pro["scores"], 1)
            sp.dma_start(tables[1][0:NPAD, :].rearrange("(b p) f -> p b f", p=P),
                         tiles(stage[:, 0:BLOCKS * TW], BLOCKS)).then_inc(table_out, 16)
            sp.dma_start(tables[1][NPAD:ACC, :], stage[:, 0:TW]).then_inc(table_out, 16)
            sp.wait_ge(table_out, 16 * TABLE_DMAS[1])
            walk(sp, general, l1["added"], [(load_indices(1), 0), (load_zd, 0)], [load_indices(1)], [load_zd], 0)
            for n in (2, 3, 4):
                write_table(n)
                walk(sp, general, lw[n]["added"], [(load_indices(n), 0)], [load_indices(n)], [], 0)
            for j in range(NJ):
                reached(sp, nd[5]["resid"], j + 1)
                last = min((j + 1) * BJ, FULL)
                sp.dma_start(out[j * BW:last * P, :].rearrange("(b p) f -> p b f", p=P),
                             tiles(X[:, j * BW:last * D], last - j * BJ)).then_inc(out_done, 16)
            if REST:
                sp.dma_start(out[FULL * P:N, :], X[0:REST, FULL * D:BLOCKS * D]).then_inc(out_done, 16)
            sp.wait_ge(out_done, 16 * (NJ + (REST > 0)))

        @block.gpsimd
        def _(pool):
            pool.memset(ident[:, :], 0.0).then_inc(pool_consts, 1)
            pool.memset(ones[:, :], 1.0).then_inc(pool_consts, 1)
            pool.iota(iota_i[:, :], pattern=[[1, P]], base=0, channel_multiplier=0).then_inc(pool_consts, 1)
            pool.iota(pidx_i[:, :], pattern=[[0, 1]], base=0, channel_multiplier=1).then_inc(pool_consts, 1)
            pool.wait_ge(pool_consts, 4)
            pool.affine_select(out=ident[:, :], in_=ident[:, :], compare_op=ALU.not_equal, fill=1.0, base=0,
                               pattern=[[-1, P]], channel_multiplier=1).then_inc(pool_consts, 1)
            pool.wait_ge(pro["viol"], 1)
            pool.partition_all_reduce(viol[:, 1:2], viol[:, 0:1], P,
                                      bass.bass_isa.ReduceOp.max).then_inc(pro["viol_all"], 1)
            pool.wait_ge(pro["flag"], 1)
            general = pool.value_load(flag_i[0:1, 0:1], min_val=0, max_val=1)

            def gather(n, slot_free):
                width = TW if n == 1 else D

                def stage_(st):
                    if not st.general and not isinstance(st.c, int):
                        pool.wait_ge(slot_free, st.c - (ROWS - 1))
                        pool.sem_inc(turns, 1)
                    indices_ready(pool, n, st)
                    pool.sem_inc(turns, 1)
                    for t in range(TILES):
                        pool.indirect_dma_start(
                            G[st.r][:, t * width:(t + 1) * width], None, tables[n],
                            bass.IndirectOffsetOnAxis(ap=idx[st.r][:, t:t + 1], axis=0)).then_inc(rows_in[st.r], 16)
                return stage_

            def gather_rows(st):
                ready(pool, l0["gidx"], st)
                pool.sem_inc(turns, 1)
                for t in range(TILES):
                    pool.indirect_dma_start(
                        G[st.r][:, t * D:(t + 1) * D], None, tables[0],
                        bass.IndirectOffsetOnAxis(ap=gather_idx[:, t:t + 1], axis=0)).then_inc(l0["gathered"], 16)

            def scatter(st):
                ready(pool, l0["idx"], st)
                pool.sem_inc(turns, 1)
                ready(pool, l0["out"], st)
                pool.sem_inc(turns, 1)
                for t in range(TILES):
                    if not (t < SUMS and (st.general or isinstance(st.c, int) and st.c == 0)):
                        pool.wait_ge(summed[t % SUMS], st.c * (16 * TILES // SUMS) + 16 * (t // SUMS))
                        pool.sem_inc(turns, 1)
                    pool.indirect_dma_start(
                        sums_dram[t % SUMS], bass.IndirectOffsetOnAxis(ap=idx[st.r][:, t:t + 1], axis=0),
                        G[st.r][:, t * D:(t + 1) * D], None, compute_op=ALU.add).then_inc(summed[t % SUMS], 16)

            def chunk_over(st):
                for q in range(SUMS):
                    pool.wait_ge(summed[q], (st.c + 1) * (16 * TILES // SUMS))
                    pool.sem_inc(turns, 1)
                pool.sem_inc(l0["over"], 1)

            pool.wait_ge(table_out, 16 * TABLE_DMAS[0])
            pool.wait_ge(sums_clear, 16 * SUMS)
            walk(pool, general, l0["over"], [(scatter, 1)], [gather_rows, scatter, chunk_over], [], 1, credit=True, steps=1)
            for q in range(SUMS):
                pool.wait_ge(summed[q], CHUNKS * 16 * TILES // SUMS)
            pool.sem_inc(all_summed, 1)

            frees = [None, l1["nm"], lw[2]["sums"], lw[3]["sums"], lw[4]["sums"]]
            overs = [None, l1["added"], lw[2]["added"], lw[3]["added"], lw[4]["added"]]
            for n in range(1, 5):
                if n == 1:
                    pool.wait_ge(pro["gmin"], 1)
                    pool.partition_all_reduce(gmin[:, 1:2], gmin[:, 0:1], P,
                                              bass.bass_isa.ReduceOp.max).then_inc(pro["gmin_all"], 1)
                pool.wait_ge(table_out, 16 * TABLE_DMAS[n])
                pool.wait_ge(acc_ready, n)
                g = gather(n, frees[n])
                walk(pool, general, overs[n], [(g, 0)], [g], [], 0)

        @block.scalar
        def _(act):
            A = nc.scalar

            def normalized(n, to_stage=False):
                def body(j):
                    s = nd[n]
                    if not to_stage:
                        batch_before(act, s["tr"] if n in (0, 3) else s["rows"], j)
                        if n == 3:
                            batch_before(act, s["rows"], j)
                    for b in range(BJ):
                        at = bass.ds(j * BW + b * D, D)
                        to = stage[:, at] if to_stage else h7[:, b * D:(b + 1) * D]
                        ins = A.activation(to, X[:, at], ACT.Relu,
                                           bias=col["bias"][:, bass.ds(j * BJ + b, 1)],
                                           scale=col["scale"][:, bass.ds(j * BJ + b, 1)])
                    ins.then_inc((s["rows"] if to_stage else s["h"]).sem, 1)
                return body

            def turned_to_lhs(n):
                def body(j):
                    reached(act, nd[n]["tr"], j + 1)
                    batch_before(act, nd[n]["prod"], j)
                    A.copy(lhs7, psA[:, 0:BW]).then_inc(nd[n]["lhs"].sem, 1)
                return body

            def turned_to_acc(n):
                def body(j):
                    reached(act, nd[n]["tr"], j + 1)
                    act.sem_inc(turns, 1)
                    A.copy(acc[:, batch(j)], psA[:, 0:BW]).then_inc(nd[n]["turned"].sem, 1)
                return body

            def acc_to_lhs(n):
                def body(j):
                    batch_before(act, nd[n]["prod"], j)
                    act.sem_inc(turns, 1)
                    A.copy(lhs7, acc[:, batch(j)]).then_inc(nd[n]["lhs"].sem, 1)
                return body

            def sqrt_of(n):
                reached(act, nd[n]["stats"], 1)
                A.activation(col["std"][:, :], col["var"][:, :], ACT.Sqrt).then_inc(nd[n]["std"].sem, 1)
                reached(act, nd[n]["cols"], 1)

            def roots_of_degrees(n):
                reached(act, nd[n]["deg"], 1)
                A.activation(degroot[:, :], deg[:, :], ACT.Sqrt).then_inc(nd[n]["root"].sem, 1)

            act.wait_ge(pro["mix_max"], 1)
            A.activation(mix[:, 3:6], mix[:, 0:3], ACT.Exp, bias=mix[:, 6:7]).then_inc(pro["mix_exp"], 1)
            sqrt_of(0)
            rows_of, lhs_of = normalized(0), turned_to_lhs(0)
            batches(act, lambda j: (rows_of(j), lhs_of(j)))
            act.wait_ge(pro["flag"], 1)
            general = act.value_load(flag_i[0:1, 0:1], min_val=0, max_val=1)

            def filter_ssp(st):
                ready(act, l0["pre"], st)
                done_before(act, l0["ssp"], st, 1)
                A.activation(big[2][:, :], psA[:, :], ACT.Abs, bias=bf1[:, 0:1]).then_inc(l0["abs"], 1)
                A.activation(big[0][:, :], psA[:, :], ACT.Relu, bias=bf1[:, 0:1]).then_inc(l0["relu"], 1)
                ready(act, l0["abs"], st)
                A.activation(big[3][:, :], big[2][:, :], ACT.Exp, scale=-1.0).then_inc(l0["exp"], 1)
                ready(act, l0["exp"], st)
                A.activation(big[1][:, :], big[3][:, :], ACT.Ln, scale=0.5, bias=half[:, 0:1]).then_inc(l0["ln"], 1)

            def rows_kept(st):
                ready(act, l0["rows"], st)
                if not isinstance(st.c, int) or st.c >= ROWS:
                    for q in range(SUMS):
                        act.wait_ge(summed[q], (st.c - (ROWS - 1)) * (16 * TILES // SUMS))
                A.copy(G[st.r][:, 0:CHUNK // 2], psC[:, :]).then_inc(l0["rows_low"], 1)
                A.copy(G[st.r][:, CHUNK // 2:CHUNK], psD[:, :]).then_inc(l0["rows_high"], 1)

            def sums_kept(st):
                ready(act, l0["summed"], st)
                A.copy(G[st.r][:, 0:CHUNK // 2], psE[:, :]).then_inc(l0["out_low"], 1)
                A.copy(G[st.r][:, CHUNK // 2:CHUNK], psF[:, :]).then_inc(l0["out"], 1)

            act.wait_ge(begun, 1)
            act.preload_act_table_set("natural_log_exp_and_others")
            walk(act, general, l0["over"], [(filter_ssp, 0), (rows_kept, 0), (sums_kept, 1)], [filter_ssp, sums_kept], [], 1,
                 steps=1)

            batches(act, turned_to_acc(1))

            act.wait_ge(acc_ready, 1)
            s = nd[1]

            def output_ssp(j):
                reached(act, s["mm"], j + 1)
                batch_before(act, s["lhs"], j)
                ps = tiles(psA[:, :], 2)[:, :, 0:HALF]
                A.activation(tiles(t7, 2), ps, ACT.Abs, bias=bo1[:, 0:1]).then_inc(s["abs"].sem, 1)
                A.activation(tiles(h7, 2), ps, ACT.Relu, bias=bo1[:, 0:1]).then_inc(s["relu"].sem, 1)
                reached(act, s["abs"], j + 1)
                A.activation(u7, t7, ACT.Exp, scale=-1.0).then_inc(s["exp"].sem, 1)
                reached(act, s["exp"], j + 1)
                A.activation(v7, u7, ACT.Ln, scale=0.5, bias=half[:, 0:1]).then_inc(s["ln"].sem, 1)

            batches(act, output_ssp)
            sqrt_of(1)
            batches(act, normalized(1))

            def diagonals(st):
                rows_ready(act, 1, st)
                done_before(act, l1["masked"], st, 1)
                for t in range(TILES):
                    ins = A.activation(big[0][:, t * P:(t + 1) * P], ident[:, :], ACT.Copy,
                                       scale=G[st.r][:, t * TW + ZS:t * TW + ZS + 1])
                ins.then_inc(l1["diag"], 1)

            def onehot_turned(st):
                ready(act, l1["masked"], st)
                done_before(act, l1["edge"], st, 2)
                A.activation(big[1 + slot(st)][:, :], psA[:, :], ACT.Sign).then_inc(l1["st"], 1)

            def exps(st):
                ready(act, l1["arg"], st)
                A.activation(small["ex"][slot(st)][:, :], small["b"][slot(st)][:, :], ACT.Exp).then_inc(l1["ex"], 1)
                ready(act, l1["decay_arg"], st)
                A.activation(decay[slot(st)][:, :], decay[slot(st)][:, :], ACT.Exp).then_inc(l1["decay"], 1)

            def node_sums(st):
                ready(act, l1["nm"], st)
                done_before(act, l1["tr"], st, 1)
                A.copy(nm_sb[:, 0:D + 1], psE[:, 0:D + 1]).then_inc(l1["nm_sb"], 1)

            act.wait_ge(begun, 2)
            act.preload_act_table_set("exp_and_others")
            walk(act, general, l1["added"], [(diagonals, 0), (exps, 1), (onehot_turned, 0), (node_sums, 2)],
                 [], [diagonals, onehot_turned, exps, node_sums], 2)

            roots_of_degrees(2)
            sqrt_of(2)
            batches(act, normalized(2, to_stage=True))
            act.wait_ge(acc_ready, 3)
            roots_of_degrees(3)
            batches(act, acc_to_lhs(3))
            sqrt_of(3)
            rows_of, acc_of = normalized(3), turned_to_acc(3)
            batches(act, lambda j: (rows_of(j), acc_of(j)))
            act.wait_ge(acc_ready, 4)
            lhs_of, acc_of4 = acc_to_lhs(4), turned_to_acc(4)
            batches(act, lambda j: (lhs_of(j), acc_of4(j)))
            act.wait_ge(acc_ready, 5)
            batches(act, acc_to_lhs(5))

        @block.tensor
        def _(pe):
            M = nc.tensor

            def batch_transposes(n, j):
                s = nd[n]
                reached(pe, s["h"], j + 1)
                batch_before(pe, s["lhs"] if n == 0 else s["turned"], j)
                for b in range(BJ):
                    ins = M.transpose(psA[:, b * P:(b + 1) * P], h7[:, b * D:(b + 1) * D], ident[:, :])
                ins.then_inc(s["tr"].sem, 1)

            def batch_products(n, w, j):
                s = nd[n]
                reached(pe, s["lhs"], j + 1)
                batch_before(pe, s["rows"] if n == 0 else s["upd"], j)
                for b in range(BJ):
                    ins = M.matmul(psB[:, b * D:(b + 1) * D], lhs7[:, b * P:(b + 1) * P], w[:, :],
                                   start=True, stop=True)
                ins.then_inc(s["prod"].sem, 1)

            pe.wait_ge(pool_consts, 5)
            pe.wait_ge(pro["dst"], 1)
            M.matmul(psC[:, 0:CHUNKS], ones[0:1, :], dst[0:1, :].rearrange("p (c t) -> p c t", t=TILES)[:, :, 0],
                     start=True, stop=True).then_inc(pro["first_row"], 1)
            pe.wait_ge(pro["vdiag"], 1)
            M.matmul(psD[:, 0:P], ones[:, :], tmp[0][:, :], start=True, stop=True)
            M.matmul(psE[:, 0:P], ones[:, :], tmp[1][:, :], start=True, stop=True).then_inc(pro["vrow"], 1)
            batches(pe, lambda j: (batch_transposes(0, j), batch_products(0, W["in"], j)))
            pe.wait_ge(pro["flag"], 1)
            general = pe.value_load(flag_i[0:1, 0:1], min_val=0, max_val=1)

            def filter_one(st):
                pe.wait_ge(rows_at[st.k], 48 * (st.turn2 + 1))
                done_before(pe, l0["relu"], st, 1)
                for q in range(2):
                    ins = M.matmul(psA[:, q * 512:(q + 1) * 512], wf1[:, :], attr[st.k][:, q * 512:(q + 1) * 512],
                                   start=True, stop=True)
                ins.then_inc(l0["pre"], 1)

            def window_rows(st):
                ready(pe, l0["spread"], st)
                pe.wait_ge(h_in[st.k], 16 * (st.turn2 + 1))
                done_before(pe, l0["rows_high"], st, 1)
                for t in range(TILES):
                    half_bank = (psC, psD)[t // (TILES // 2)]
                    at = t % (TILES // 2) * D
                    ins = M.matmul(half_bank[:, at:at + D], S[st.k][:, t * P:(t + 1) * P], h_win[st.k][:, :],
                                   start=True, stop=True)
                ins.then_inc(l0["rows"], 1)

            def filter_two(st):
                ready(pe, l0["ssp"], st)
                done_before(pe, l0["msg"], st, 1)
                for t in range(TILES):
                    M.matmul(psB[:, t * D:(t + 1) * D], ones16[:, :], bf2_rows[:, :], start=True, stop=False)
                    ins = M.matmul(psB[:, t * D:(t + 1) * D], big[4][:, t * P:(t + 1) * P], W["f2"][:, :],
                                   start=False, stop=True)
                ins.then_inc(l0["wij"], 1)

            def source_counts(st):
                pe.wait_ge(l1["hot"], st.c + 1)
                done_before(pe, l1["counted"], st, 1)
                for t in range(TILES):
                    ins = M.matmul(psB[:, 0:BLOCKS], lohot[:, t * P:(t + 1) * P],
                                   hihot[:, t * BLOCKS:(t + 1) * BLOCKS], start=(t == 0), stop=(t == TILES - 1))
                ins.then_inc(l1["hist"], 1)

            def equal_sources_summed(st):
                ready(pe, l0["same"], st)
                ready(pe, l0["msg"], st)
                done_before(pe, l0["out"], st, 1)
                for t in range(TILES):
                    half_bank = (psE, psF)[t // (TILES // 2)]
                    at = t % (TILES // 2) * D
                    ins = M.matmul(half_bank[:, at:at + D], same[st.k][:, t * P:(t + 1) * P],
                                   msg[st.k][:, t * D:(t + 1) * D], start=True, stop=True)
                ins.then_inc(l0["summed"], 1)

            pe.wait_ge(begun, 1)
            walk(pe, general, l0["over"],
                 [(filter_one, 0), (filter_two, 1), (window_rows, 0), (equal_sources_summed, 1)],
                 [filter_one, filter_two, equal_sources_summed], [], 1, steps=1)

            def sums_turned_to_acc(j):
                pe.wait_ge(sums_in, 16 * SUMS * (j + 1))
                batch_before(pe, nd[1]["turned"], j)
                for b in range(BJ):
                    for q in range(SUMS):
                        ins = M.matmul(psA[:, b * P:(b + 1) * P], G[q][:, b * D:(b + 1) * D], ident[:, :],
                                       start=(q == 0), stop=(q == SUMS - 1))
                ins.then_inc(nd[1]["tr"].sem, 1)
            batches(pe, sums_turned_to_acc)

            s = nd[1]
            pe.wait_ge(acc_ready, 1)

            def output_network(j):
                batch_before(pe, s["relu"], j)
                for q in range(2):
                    ins = M.matmul(psA[:, q * 512:q * 512 + HALF], W["o1"][:, :],
                                   acc[:, bass.ds(j * BW + q * HALF, HALF)], start=True, stop=True)
                ins.then_inc(s["mm"].sem, 1)
                batch_products(1, W["o2"], j)

            batches(pe, output_network)

            def masked_scores(st):
                ready(pe, l1["onehot"], st)
                ready(pe, l1["diag"], st)
                done_before(pe, l1["mx"], st, 1)
                for t in range(TILES):
                    ins = M.matmul(psA[:, t * P:(t + 1) * P], hot(st)[:, t * P:(t + 1) * P],
                                   big[0][:, t * P:(t + 1) * P], start=True, stop=True)
                ins.then_inc(l1["masked"], 1)

            def per_edge(st):
                ready(pe, l1["pair"], st)
                ready(pe, l1["st"], st)
                done_before(pe, l1["arg"], st, 1)
                for t in range(TILES):
                    ins = M.matmul(psC[:, 2 * t:2 * t + 2], big[1 + slot(st)][:, t * P:(t + 1) * P],
                                   mcol["pair"][slot(st)][:, 0:2], start=True, stop=True)
                ins.then_inc(l1["edge"], 1)
                ready(pe, l1["top_diag"], st)
                done_before(pe, l1["top_new"], st, 1)
                M.matmul(psD[:, 0:P], ones[:, :], top_diag[:, :], start=True, stop=True).then_inc(l1["toprow"], 1)

            def weighted_rows(st):
                ready(pe, l1["weights"], st)
                done_before(pe, l1["nm_sb"], st, 1)
                for t in range(TILES):
                    ins = M.matmul(psE[:, 0:D + 1], hot(st)[:, t * P:(t + 1) * P],
                                   G[st.r][:, t * TW:t * TW + D + 1], start=(t == 0), stop=(t == TILES - 1))
                ins.then_inc(l1["nm"], 1)

            def sums_turned(st):
                ready(pe, l1["nm_sb"], st)
                done_before(pe, l1["added"], st, 1)
                M.matmul(psF[:, 0:P], nm_sb[:, 0:D], ident[:, :], start=True, stop=True)
                M.matmul(psF[:, P:2 * P], nm_sb[:, D:D + 1].to_broadcast([P, P]), ident[:, :],
                         start=True, stop=True).then_inc(l1["tr"], 1)

            pe.wait_ge(begun, 2)
            walk(pe, general, l1["added"], [(sums_turned, 3), (per_edge, 1), (masked_scores, 0), (weighted_rows, 2),
                                           (source_counts, 0)],
                 [source_counts], [masked_scores, per_edge, weighted_rows, sums_turned], 3)

            def weighted_pass(n):
                s = lw[n]

                def sums(st):
                    ready(pe, s["onehot"], st)
                    rows_ready(pe, n, st)
                    done_before(pe, s["added"], st, 2)
                    if n == 2:
                        ready(pe, s["ones"], st)
                        for t in range(TILES):
                            M.matmul(bank(st)[0:2, P:2 * P], onesew[slot(st)][:, 2 * t:2 * t + 2],
                                     S[slot(st)][:, t * P:(t + 1) * P], start=(t == 0), stop=(t == TILES - 1))
                    for t in range(TILES):
                        ins = M.matmul(bank(st)[:, 0:P], G[st.r][:, t * D:(t + 1) * D],
                                       S[slot(st)][:, t * P:(t + 1) * P], start=(t == 0), stop=(t == TILES - 1))
                    ins.then_inc(s["sums"], 1)

                pe.wait_ge(begun, n + 1)
                walk(pe, general, s["added"], [(sums, 0)], [], [sums], 0)

            pe.wait_ge(acc_ready, 2)
            batches(pe, lambda j: batch_products(2, W["gat"], j))
            weighted_pass(2)
            pe.wait_ge(acc_ready, 3)
            for b in range(BLOCKS):
                ins = M.matmul(psC[:, 2 * b:2 * b + 2], degrow[0:2, b * P:(b + 1) * P], ident[0:2, 0:2],
                               start=True, stop=True)
            ins.then_inc(nd[3]["counts"].sem, 1)
            batches(pe, lambda j: batch_products(3, W["gc"], j))
            batches(pe, lambda j: batch_transposes(3, j))
            weighted_pass(3)
            pe.wait_ge(acc_ready, 4)
            batches(pe, lambda j: (batch_products(4, W["g0"], j), batch_transposes(4, j)))
            weighted_pass(4)
            pe.wait_ge(acc_ready, 5)
            batches(pe, lambda j: batch_products(5, W["g1"], j))

        @block.vector
        def _(dve):
            V = nc.vector
            if REST:
                V.memset(X[:, FULL * D:BLOCKS * D], 0.0).then_inc(x_tail, 1)
            V.memset(half[:, :], 0.5)
            V.memset(hist[:, :], 0.0)
            V.memset(acc[:, :], 0.0).then_inc(zeroed, 1)
            dve.wait_ge(loaded, 16 * (len(LOADS) + 1 + (REST > 0)))
            dve.wait_ge(pool_consts, 5)
            link(V.tensor_copy(dst[:, :], dst_i[:, :]))
            dve.sem_inc(pro["dst"], 1)
            link(V.tensor_copy(iota[:, :], iota_i[:, :]))
            link(V.tensor_copy(srcf[:, :], src_i[:, :]))
            link(V.tensor_copy(pidx[:, :], pidx_i[:, :]))
            V.tensor_scalar(tri[:, :], iota[:, :], pidx[:, 0:1], None, ALU.is_lt)
            V.tensor_scalar(trash[:, :], pidx[:, :], float(NPAD), None, ALU.add)
            V.memset(ones16[:, :], 1.0)
            link(V.tensor_copy(bf2_part[0][:, :], rowb["bf2"][:, :]))
            link(V.tensor_tensor(tmp[2][:, :], rowb["bf2"][:, :], bf2_part[0][:, :], ALU.subtract))
            link(V.tensor_copy(bf2_part[1][:, :], tmp[2][:, :]))
            link(V.tensor_tensor(tmp[3][:, :], tmp[2][:, :], bf2_part[1][:, :], ALU.subtract))
            link(V.tensor_copy(bf2_part[2][:, :], tmp[3][:, :]))
            link(V.tensor_scalar(bf2_rows[:, :], bf2_part[0][:, :], ident[:, 0:1], None, ALU.mult))
            for k in (1, 2):
                link(V.scalar_tensor_tensor(out=bf2_rows[:, :], in0=bf2_part[k][:, :], scalar=ident[:, k:k + 1],
                                            in1=bf2_rows[:, :], op0=ALU.mult, op1=ALU.add))
            link(V.tensor_scalar(big_i[:, 0:E_COLS], src_i[:, :], 7, None, ALU.arith_shift_right))
            link(V.tensor_copy(srch[:, :], big_i[:, 0:E_COLS]))
            link(V.tensor_scalar(far[1], dst[:, :], 0.0, None, ALU.is_ge))
            link(V.scalar_tensor_tensor(out=far[2], in0=srch[:, :], scalar=1.0, in1=far[1], op0=ALU.add, op1=ALU.mult))
            link(V.tensor_scalar(srch[:, :], far[2], -1.0, None, ALU.add))
            link(V.tensor_scalar(big_i[:, 0:E_COLS], src_i[:, :], P - 1, None, ALU.bitwise_and))
            link(V.tensor_copy(srcl[:, :], big_i[:, 0:E_COLS]))
            V.tensor_scalar(wbase[:, :], iota[:, 0:BLOCKS], float(P), None, ALU.mult)
            V.tensor_tensor_reduce(tmp[2][:, :], W["gat"][:, :], rowb["asrc"][:, :], 1.0, 0.0, ALU.mult, ALU.add,
                                   vcol[:, 0:1])
            link(V.tensor_tensor_reduce(tmp[3][:, :], W["gat"][:, :], rowb["adst"][:, :], 1.0, 0.0, ALU.mult, ALU.add,
                                        vcol[:, 1:2]))
            V.tensor_scalar(tmp[0][:, :], ident[:, :], vcol[:, 0:1], None, ALU.mult)
            V.tensor_scalar(tmp[1][:, :], ident[:, :], vcol[:, 1:2], None, ALU.mult).then_inc(pro["vdiag"], 1)
            link(V.tensor_reduce(mix[:, 7:8], mix[:, 0:3], AX.X, ALU.max))
            link(V.tensor_scalar(mix[:, 6:7], mix[:, 7:8], -1.0, None, ALU.mult))
            dve.sem_inc(pro["mix_max"], 1)
            dve.wait_ge(pro["vrow"], 1)
            V.tensor_copy(vsrc[:, :], psD[:, 0:P])
            V.tensor_copy(vdst[:, :], psE[:, 0:P])
            dve.wait_ge(pro["first_row"], 1)
            link(V.tensor_copy(first[:, :], psC[:, 0:CHUNKS]))
            link(V.tensor_tensor(tiles(far[0], CHUNKS), tiles(dst[:, :], CHUNKS), along(first[:, :], TILES),
                                 ALU.subtract))
            link(V.tensor_scalar(far[1], far[0], float(P - 1), None, ALU.is_gt))
            link(V.tensor_scalar(far[2], dst[:, :], 0.0, None, ALU.is_ge))
            link(V.scalar_tensor_tensor(out=far[3], in0=far[0], scalar=0.0, in1=far[2], op0=ALU.is_lt, op1=ALU.mult))
            link(V.tensor_tensor(far[2], far[3], far[1], ALU.max))
            V.tensor_reduce(viol[:, 0:1], far[2], AX.X, ALU.max).then_inc(pro["viol"], 1)
            dve.wait_ge(pro["mix_exp"], 1)
            link(V.tensor_reduce(mix[:, 7:8], mix[:, 3:6], AX.X, ALU.add))
            link(V.reciprocal(mix[:, 6:7], mix[:, 7:8]))
            link(V.tensor_scalar(mix[:, 0:3], mix[:, 3:6], mix[:, 6:7], None, ALU.mult))
            link(V.tensor_reduce(csum[:, :], mix[:, 0:3], AX.X, ALU.add))
            dve.wait_ge(pro["viol_all"], 1)
            V.tensor_copy(flag_i[:, :], viol[:, 1:2]).then_inc(pro["flag"], 1)

            def block_stats(j):
                for b in range(BJ):
                    ins = V.bn_stats(stat[:, bass.ds(j * (BJ * 6) + b * 6, 6)], X[:, bass.ds(j * BW + b * D, D)])
                return ins

            def norm_columns(n, factor=None):
                q = stat[:, :].rearrange("p (b s) -> p b s", s=6)
                c = {k: v[:, :] for k, v in col.items()}
                link(V.tensor_tensor(c["mean"], q[:, :, 1], q[:, :, 4], ALU.add))
                link(V.tensor_tensor(c["diff"], q[:, :, 1], q[:, :, 4], ALU.subtract))
                link(V.tensor_tensor(c["t0"], c["diff"], c["diff"], ALU.mult))
                link(V.tensor_tensor(c["t1"], q[:, :, 2], q[:, :, 5], ALU.add))
                link(V.tensor_scalar(c["var"], c["t1"], 1.0 / D, EPS, ALU.mult, ALU.add))
                V.scalar_tensor_tensor(out=c["var"], in0=c["t0"], scalar=0.25, in1=c["var"], op0=ALU.mult,
                                       op1=ALU.add).then_inc(nd[n]["stats"].sem, 1)
                reached(dve, nd[n]["std"], 1)
                link(V.reciprocal(c["rstd"], c["std"]))
                if factor is None:
                    link(V.tensor_copy(c["scale"], c["rstd"]))
                else:
                    link(V.tensor_tensor(c["scale"], c["rstd"], factor, ALU.mult))
                V.scalar_tensor_tensor(out=c["bias"], in0=c["mean"], scalar=-0.5, in1=c["scale"], op0=ALU.mult,
                                       op1=ALU.mult).then_inc(nd[n]["cols"].sem, 1)

            def start_pass(n, last, clear=()):
                for name in last.split():
                    reached(dve, nd[n][name], NJ)
                for buffer, value in clear:
                    V.memset(buffer, value)
                links.base += 1
                V.memset(viol[:, 2:3], 0.0).then_inc(dve_link, 1)
                dve.wait_ge(dve_link, links.base)
                dve.sem_inc(begun, 1)

            def local_dst(st, s):
                base = first[:, bass.ds(st.c, 1)] if st.w is None else wbase[:, bass.ds(st.w, 1)]
                V.tensor_scalar(dloc[slot(st)][:, :], dst[:, st.cols], base, None, ALU.subtract).then_inc(s["dloc"], 1)

            def onehot(st, s, reader, to, depth=2):
                ready(dve, s["dloc"], st)
                done_before(dve, reader, st, depth)
                V.tensor_tensor(tiles(to[:, :]), over_tiles(iota[:, :]), along(dloc[slot(st)][:, :], P),
                                ALU.is_equal).then_inc(s["onehot"], 1)

            def add_sums(st, s):
                ready(dve, s["sums"], st)
                done_before(dve, s["added"], st, 1)
                at = bass.ds(window(dve, st), P)
                V.tensor_tensor(acc[:, at], acc[:, at], bank(st)[:, 0:P], ALU.add).then_inc(s["added"], 1)

            with dve.Fori(0, NJ) as j:
                block_stats(j).then_inc(nd[0]["bn"].sem, 1)
            reached(dve, nd[0]["bn"], NJ)
            norm_columns(0)

            def table_rows_0(j):
                reached(dve, nd[0]["prod"], j + 1)
                V.tensor_copy(stage[:, batch(j)], psB[:, 0:BW]).then_inc(nd[0]["rows"].sem, 1)
            batches(dve, table_rows_0)
            start_pass(0, "rows")
            general = dve.value_load(flag_i[0:1, 0:1], min_val=0, max_val=1)

            def filter_sum(st):
                ready(dve, l0["relu"], st)
                ready(dve, l0["ln"], st)
                done_before(dve, l0["wij"], st, 1)
                V.tensor_tensor(big[4][:, :], big[0][:, :], big[1][:, :], ALU.add).then_inc(l0["ssp"], 1)

            def spread_window(st):
                V.tensor_tensor(node_id[st.k][:, :], pidx[:, :], first[:, bass.ds(st.c, 1)],
                                ALU.add).then_inc(l0["node_id"], 1)
                dve.wait_ge(rows_at[st.k], 48 * (st.turn2 + 1))
                done_before(dve, l0["rows"], st, 2)
                ready(dve, l0["node_id"], st)
                V.tensor_scalar(S[st.k][:, :], dst_row[st.k], node_id[st.k][:, 0:1], None,
                                ALU.is_equal).then_inc(l0["spread"], 1)

            def gather_indices(st):
                V.tensor_scalar(gather_f[:, :], dst[:, st.cols], 0.0, None, ALU.max).then_inc(l0["gidx_f"], 1)
                ready(dve, l0["gidx_f"], st)
                V.tensor_copy(gather_idx[:, :], gather_f[:, :]).then_inc(l0["gidx"], 1)

            def same_source(st):
                dve.wait_ge(rows_at[st.k], 48 * (st.turn2 + 1))
                done_before(dve, l0["summed"], st, 2)
                for t in range(TILES):
                    at = bass.ds(st.c * TILES + t, 1)
                    ins = V.tensor_scalar(same[st.k][:, t * P:(t + 1) * P], src_row[st.k][:, t * P:(t + 1) * P],
                                          srcf[:, at], cut[:, at], ALU.is_equal, ALU.mult)
                ins.then_inc(l0["same"], 1)

            def scatter_indices(st):
                done_before(dve, l0["away"], st, 1)
                for t in range(TILES):
                    at = bass.ds(st.c * TILES + t, 1)
                    ins = V.scalar_tensor_tensor(
                        out=earlier[:, t * P:(t + 1) * P], in0=src_row[st.k][:, t * P:(t + 1) * P],
                        scalar=srcf[:, at], in1=tri[:, :], op0=ALU.is_equal, op1=ALU.mult,
                        accum_out=dup["count"][:, t:t + 1])
                ins.then_inc(l0["compared"], 1)
                ready(dve, l0["compared"], st)
                V.tensor_scalar(dup["is"][:, :], dup["count"][:, :], 0.0, None, ALU.is_gt)
                V.tensor_scalar(dup["away"][:, :], srcf[:, st.cols], trash[:, 0:1], -1.0, ALU.subtract,
                                ALU.mult).then_inc(l0["away"], 1)
                ready(dve, l0["away"], st)
                V.tensor_tensor(dup["to"][:, :], dup["is"][:, :], dup["away"][:, :], ALU.mult).then_inc(l0["moved"], 1)
                ready(dve, l0["moved"], st)
                V.tensor_tensor(dup["is"][:, :], dup["to"][:, :], srcf[:, st.cols], ALU.add).then_inc(l0["to"], 1)
                ready(dve, l0["to"], st)
                if not st.general and not (isinstance(st.c, int) and st.c < ROWS):
                    for q in range(SUMS):
                        dve.wait_ge(summed[q], (st.c - (ROWS - 1)) * (16 * TILES // SUMS))
                V.tensor_copy(idx[st.r][:, :], dup["is"][:, :]).then_inc(l0["idx"], 1)

            def messages(st):
                ready(dve, l0["wij"], st)
                if st.general:
                    dve.wait_ge(l0["gathered"], 16 * TILES * (st.c + 1))
                else:
                    ready(dve, l0["rows_high"], st)
                done_before(dve, l0["summed"], st, 2)
                V.tensor_tensor(msg[st.k], psB[:, :], G[st.r][:, 0:CHUNK], ALU.mult).then_inc(l0["msg"], 1)

            def weighted_onehot(s, weight):
                def stage_(st):
                    local_dst(st, s)
                    ready(dve, s["dloc"], st)
                    done_before(dve, s["sums"], st, 2)
                    for t in range(TILES):
                        ins = V.tensor_scalar(S[slot(st)][:, t * P:(t + 1) * P], iota[:, :],
                                              dloc[slot(st)][:, t:t + 1], weight[:, bass.ds(st.c * TILES + t, 1)],
                                              ALU.is_equal, ALU.mult)
                    ins.then_inc(s["onehot"], 1)
                return stage_

            walk(dve, general, l0["over"],
                 [(filter_sum, 1), (spread_window, 0), (same_source, 1), (messages, 1), (scatter_indices, 1)],
                 [gather_indices, filter_sum, messages, same_source, scatter_indices], [], 1, steps=1)
            reached(dve, nd[1]["turned"], NJ)
            dve.sem_inc(acc_ready, 1)

            s1 = nd[1]

            def node_1(j):
                reached(dve, s1["ln"], j + 1)
                reached(dve, s1["relu"], j + 1)
                batch_before(dve, s1["prod"], j)
                V.tensor_tensor(lhs7, h7, v7, ALU.add).then_inc(s1["lhs"].sem, 1)
                reached(dve, s1["prod"], j + 1)
                V.tensor_tensor(tiles(w7, BJ), tiles(psB[:, 0:BW], BJ), over_blocks(rowb["bo2"][:, :]),
                                ALU.add).then_inc(s1["upd"].sem, 1)
                reached(dve, s1["upd"], j + 1)
                V.tensor_tensor(X[:, batch(j)], X[:, batch(j)], w7, ALU.add).then_inc(s1["resid"].sem, 1)
                reached(dve, s1["resid"], j + 1)
                block_stats(j).then_inc(s1["bn"].sem, 1)
            batches(dve, node_1)
            reached(dve, s1["bn"], NJ)
            norm_columns(1)
            stage_t = stage[:, 0:BLOCKS * TW].rearrange("p (b w) -> p b w", w=TW)
            V.memset(stage_t[:, :, ONE:TW], 1.0)

            def scores(j):
                reached(dve, s1["h"], j + 1)
                for b in range(BJ):
                    hb = h7[:, b * D:(b + 1) * D]
                    V.tensor_tensor_reduce(t7[:, b * D:(b + 1) * D], hb, vsrc[:, :], 1.0, 0.0, ALU.mult, ALU.add,
                                           score[:, b:b + 1])
                    ins = V.tensor_tensor_reduce(u7[:, b * D:(b + 1) * D], hb, vdst[:, :], 1.0, 0.0, ALU.mult, ALU.add,
                                                 score[:, BJ + b:BJ + b + 1])
                ins.then_inc(s1["scored"].sem, 1)
                reached(dve, s1["scored"], j + 1)
                V.tensor_copy(col["zs"][:, bass.ds(j * BJ, BJ)], score[:, 0:BJ])
                V.tensor_copy(col["zd"][:, bass.ds(j * BJ, BJ)], score[:, BJ:2 * BJ]).then_inc(s1["kept"].sem, 1)
                V.tensor_copy(tiles(stage[:, batch(j, TW)], BJ)[:, :, 0:D], tiles(h7, BJ)).then_inc(s1["rows"].sem, 1)
            batches(dve, scores)
            reached(dve, s1["kept"], NJ)
            link(V.tensor_reduce(gmin[:, 2:3], col["zs"][:, :], AX.X, ALU.min))
            V.tensor_scalar(gmin[:, 0:1], gmin[:, 2:3], -1.0, None, ALU.mult).then_inc(pro["gmin"], 1)
            dve.wait_ge(pro["gmin_all"], 1)
            link(V.tensor_scalar(stage_t[:, :, ZS], col["zs"][:, :], gmin[:, 1:2], 1.0, ALU.add, ALU.add))
            link(V.tensor_scalar(stage_t[:, :, ZD], col["zd"][:, :], gmin[:, 1:2], 1.0, ALU.subtract, ALU.subtract))
            dve.sem_inc(pro["scores"], 1)
            dve.wait_ge(table_out, 16 * TABLE_DMAS[1])
            start_pass(1, "rows kept", [(acc[:, :], 0.0), (den, 0.0), (top[:, :], -3.0e38)])

            def source_hots(st):
                done_before(dve, l1["hist"], st, 1)
                V.tensor_tensor(tiles(lohot[:, :]), over_tiles(iota[:, :]), along(srcl[:, st.cols], P), ALU.is_equal)
                V.tensor_tensor(tiles(hihot[:, :]), over_tiles(iota[:, 0:BLOCKS]), along(srch[:, st.cols], BLOCKS),
                                ALU.is_equal).then_inc(l1["hot"], 1)

            def count_sources(st):
                ready(dve, l1["hist"], st)
                done_before(dve, l1["counted"], st, 1)
                V.tensor_tensor(hist[:, :], hist[:, :], psB[:, 0:BLOCKS], ALU.add).then_inc(l1["counted"], 1)
                if st.general:
                    ready(dve, l1["counted"], st)
                    dve.sem_inc(turns, 1)

            def window_onehot(st):
                local_dst(st, l1)
                onehot(st, l1, l1["nm"], hot(st), ROWS)

            def largest(st):
                ready(dve, l1["st"], st)
                V.tensor_reduce(mcol["mx"][slot(st)][:, 0:1], psA[:, :], AX.X, ALU.max).then_inc(l1["mx"], 1)

            held = {}

            def new_maxima(st):
                k = slot(st)
                done_before(dve, l1["top_new"], st, 1)
                at = bass.ds(window(dve, st), P)
                held["window"] = at
                V.tensor_copy(top_old[:, :], top[:, at]).then_inc(l1["old_row"], 1)
                if st.w is None:
                    dve.wait_ge(zd_in[k], 16 * (st.turn2 + 1))
                else:
                    dve.wait_ge(zd_in[0], 16 * (st.s + 1))
                ready(dve, l1["mx"], st)
                V.tensor_tensor(mcol["t"][k][:, 0:1], mcol["mx"][k][:, 0:1], mcol["zd"][k][:, 0:1],
                                ALU.add).then_inc(l1["t1"], 1)
                ready(dve, l1["old_row"], st)
                V.tensor_tensor_reduce(tmp[4][:, :], top_old[:, :], ident[:, :], 1.0, 0.0, ALU.mult, ALU.add,
                                       mcol["old"][k][:, 0:1]).then_inc(l1["old_col"], 1)
                ready(dve, l1["t1"], st)
                V.scalar_tensor_tensor(out=mcol["l"][k][:, 0:1], in0=mcol["t"][k][:, 0:1], scalar=SLOPE_GAT,
                                       in1=mcol["t"][k][:, 0:1], op0=ALU.mult, op1=ALU.max).then_inc(l1["t2"], 1)
                done_before(dve, l1["edge"], st, 2)
                V.tensor_copy(mcol["pair"][k][:, 0:1], mcol["zd"][k][:, 0:1])
                ready(dve, l1["t2"], st)
                ready(dve, l1["old_col"], st)
                V.tensor_tensor(mcol["pair"][k][:, 1:2], mcol["l"][k][:, 0:1], mcol["old"][k][:, 0:1],
                                ALU.max).then_inc(l1["pair"], 1)
                ready(dve, l1["pair"], st)
                done_before(dve, l1["toprow"], st, 1)
                V.tensor_scalar(top_diag[:, :], ident[:, :], mcol["pair"][k][:, 1:2], None,
                                ALU.mult).then_inc(l1["top_diag"], 1)

            def exponents(st):
                k = slot(st)
                e = psC[:, 0:2 * TILES].rearrange("p (t o) -> p t o", o=2)
                ready(dve, l1["edge"], st)
                V.tensor_tensor(small["zde"][k][:, :], tiles(G[st.r][:, :])[:, :, ZS], e[:, :, 0],
                                ALU.add).then_inc(l1["zde"], 1)
                ready(dve, l1["toprow"], st)
                done_before(dve, l1["added"], st, 2)
                V.tensor_tensor(decay[k][:, :], top_old[:, :], psD[:, 0:P], ALU.subtract).then_inc(l1["decay_arg"], 1)
                ready(dve, l1["zde"], st)
                V.scalar_tensor_tensor(out=small["l"][k][:, :], in0=small["zde"][k][:, :], scalar=SLOPE_GAT,
                                       in1=small["zde"][k][:, :], op0=ALU.mult, op1=ALU.max).then_inc(l1["leak"], 1)
                V.tensor_copy(top[:, held["window"]], psD[:, 0:P]).then_inc(l1["top_new"], 1)
                ready(dve, l1["leak"], st)
                V.tensor_tensor(small["zde"][k][:, :], small["l"][k][:, :], e[:, :, 1],
                                ALU.subtract).then_inc(l1["arg0"], 1)
                ready(dve, l1["arg0"], st)
                V.tensor_scalar(small["b"][k][:, :], small["zde"][k][:, :], 0.0, None, ALU.min).then_inc(l1["arg"], 1)

            def weights(st):
                ready(dve, l1["ex"], st)
                V.tensor_tensor(tiles(hot(st)[:, :]), tiles(hot(st)[:, :]),
                                along(small["ex"][slot(st)][:, :], P), ALU.mult).then_inc(l1["weights"], 1)

            def merge(st):
                at = bass.ds(window(dve, st), P)
                ready(dve, l1["decay"], st)
                done_before(dve, l1["added"], st, 1)
                V.tensor_tensor(tmp[0][:, :], acc[:, at], decay[slot(st)][:, :], ALU.mult)
                V.tensor_tensor(tmp[1][:, :], den[:, at], decay[slot(st)][:, :], ALU.mult).then_inc(l1["scaled"], 1)
                ready(dve, l1["scaled"], st)
                ready(dve, l1["tr"], st)
                V.tensor_tensor(acc[:, at], tmp[0][:, :], psF[:, 0:P], ALU.add)
                V.tensor_tensor(den[:, at], tmp[1][:, :], psF[:, P:2 * P], ALU.add).then_inc(l1["added"], 1)

            walk(dve, general, l1["added"],
                 [(new_maxima, 1), (merge, 3), (window_onehot, 0), (weights, 2), (exponents, 1), (source_hots, 0),
                  (largest, 0), (count_sources, 0)],
                 [source_hots, count_sources], [window_onehot, largest, new_maxima, exponents, weights, merge], 3, credit=True)
            dve.wait_ge(l1["counted"], CHUNKS)
            dve.sem_inc(acc_ready, 1)

            def reciprocal_roots(n):
                links.base += 1
                V.memset(viol[:, 3:4], 0.0).then_inc(dve_link, 1)
                dve.wait_ge(dve_link, links.base)
                dve.sem_inc(nd[n]["deg"].sem, 1)
                reached(dve, nd[n]["root"], 1)
                link(V.reciprocal(dinv[:, :], degroot[:, :]))

            link(V.memset(deg[:, :], 1.0))
            link(V.tensor_scalar(deg[:, 0:BLOCKS], hist[:, :], 1.0, None, ALU.max))
            reciprocal_roots(2)
            link(V.tensor_scalar(den, den, 1e-37, None, ALU.max))
            link(V.reciprocal(den, den))
            s2 = nd[2]

            def node_2(j):
                batch_before(dve, s2["prod"], j)
                V.tensor_tensor(lhs7, acc[:, batch(j)], stage[:, batch(j)], ALU.mult).then_inc(s2["lhs"].sem, 1)
                reached(dve, s2["prod"], j + 1)
                V.tensor_tensor(X[:, batch(j)], X[:, batch(j)], psB[:, 0:BW], ALU.add).then_inc(s2["upd"].sem, 1)
                reached(dve, s2["upd"], j + 1)
                block_stats(j).then_inc(s2["bn"].sem, 1)
            batches(dve, node_2)
            reached(dve, s2["bn"], NJ)
            norm_columns(2, dinv[:, 0:BLOCKS])
            reached(dve, s2["rows"], NJ)
            for k in range(2):
                V.memset(onesew[k][:, :], 1.0)
            start_pass(2, "upd bn", [(acc[:, :], 0.0), (degrow, 0.0)])

            def counting_onehot(st):
                s = lw[2]
                local_dst(st, s)
                V.tensor_copy(onesew[slot(st)][:, :].rearrange("p (t o) -> p t o", o=2)[:, :, 1], ew[:, st.cols])\
                    .then_inc(s["ones"], 1)
                onehot(st, s, s["sums"], S[slot(st)])

            def add2(st):
                s = lw[2]
                ready(dve, s["sums"], st)
                done_before(dve, s["added"], st, 1)
                at = bass.ds(window(dve, st), P)
                V.tensor_tensor(degrow[:, at], degrow[:, at], bank(st)[0:2, P:2 * P], ALU.add)
                V.tensor_tensor(acc[:, at], acc[:, at], bank(st)[:, 0:P], ALU.add).then_inc(s["added"], 1)

            def weighted_pass(n):
                s = lw[n]
                hot = weighted_onehot(s, ew)

                def add(st):
                    add_sums(st, s)
                walk(dve, general, s["added"], [(hot, 0), (add, 1)], [], [hot, add], 1, credit=True)
                dve.sem_inc(acc_ready, 1)

            walk(dve, general, lw[2]["added"], [(counting_onehot, 0), (add2, 1)], [], [counting_onehot, add2], 1,
                 credit=True)
            dve.sem_inc(acc_ready, 1)

            s3 = nd[3]
            reached(dve, s3["counts"], 1)
            counts = psC[:, 0:2 * BLOCKS].rearrange("p (b o) -> p b o", o=2)
            V.tensor_scalar(deg[:, 0:BLOCKS], counts[:, :, 0], 1.0, None, ALU.max)
            link(V.tensor_scalar(deg[:, BLOCKS:2 * BLOCKS], counts[:, :, 1], 1.0, None, ALU.add))
            link(V.tensor_scalar(positive[:, :], deg[:, BLOCKS:2 * BLOCKS], 0.0, None, ALU.is_gt))
            link(V.tensor_scalar(deg[:, BLOCKS:2 * BLOCKS], deg[:, BLOCKS:2 * BLOCKS], 1e-30, None, ALU.max))
            reciprocal_roots(3)
            link(V.tensor_tensor(dinv[:, BLOCKS:2 * BLOCKS], dinv[:, BLOCKS:2 * BLOCKS], positive[:, :], ALU.mult))

            def scaled_and_biased(s, j, first_col, bias):
                reached(dve, s["prod"], j + 1)
                V.tensor_tensor(tiles(t7, BJ), tiles(psB[:, 0:BW], BJ),
                                along(dinv[:, bass.ds(j * BJ + first_col, BJ)], D), ALU.mult).then_inc(s["upd"].sem, 1)
                reached(dve, s["upd"], j + 1)
                V.tensor_tensor(tiles(t7, BJ), tiles(t7, BJ), over_blocks(bias[:, :]), ALU.add).then_inc(s["biased"].sem, 1)
                reached(dve, s["biased"], j + 1)

            def node_3(j):
                scaled_and_biased(s3, j, 0, rowb["gc"])
                V.scalar_tensor_tensor(out=X[:, batch(j)], in0=t7, scalar=0.0, in1=X[:, batch(j)], op0=ALU.max,
                                       op1=ALU.add).then_inc(s3["resid"].sem, 1)
                reached(dve, s3["resid"], j + 1)
                block_stats(j).then_inc(s3["bn"].sem, 1)
            batches(dve, node_3)
            reached(dve, s3["bn"], NJ)
            norm_columns(3, dinv[:, BLOCKS:2 * BLOCKS])

            def rows_to_stage(s):
                def body(j):
                    reached(dve, s["h"], j + 1)
                    V.tensor_copy(stage[:, batch(j)], h7).then_inc(s["rows"].sem, 1)
                return body
            batches(dve, rows_to_stage(s3))
            start_pass(3, "resid bn rows turned")
            weighted_pass(3)

            def prelu(s, j, bias):
                scaled_and_biased(s, j, BLOCKS, bias)
                V.scalar_tensor_tensor(out=tiles(u7, BJ), in0=tiles(t7, BJ), scalar=0.0,
                                       in1=over_blocks(rowb["slope"][:, :]), op0=ALU.min,
                                       op1=ALU.mult).then_inc(s["neg"].sem, 1)
                reached(dve, s["neg"], j + 1)
                V.scalar_tensor_tensor(out=t7, in0=t7, scalar=0.0, in1=u7, op0=ALU.max,
                                       op1=ALU.add).then_inc(s["prelu"].sem, 1)
                reached(dve, s["prelu"], j + 1)

            s4 = nd[4]

            def node_4(j):
                prelu(s4, j, rowb["b0"])
                batch_before(dve, s4["tr"], j)
                V.tensor_tensor(tiles(h7, BJ), tiles(t7, BJ), along(dinv[:, bass.ds(j * BJ + BLOCKS, BJ)], D),
                                ALU.mult).then_inc(s4["h"].sem, 1)
                rows_to_stage(s4)(j)
            batches(dve, node_4)
            start_pass(4, "rows turned")
            weighted_pass(4)

            def node_5(j):
                batch_before(dve, nd[5]["resid"], j)
                prelu(nd[5], j, rowb["b1"])
                V.scalar_tensor_tensor(out=X[:, batch(j)], in0=t7, scalar=csum[:, 0:1], in1=X[:, batch(j)],
                                       op0=ALU.mult, op1=ALU.add).then_inc(nd[5]["resid"].sem, 1)
            batches(dve, node_5)


def kernel(**inputs):
    import concourse.bacc as bacc
    from concourse.bass_utils import run_bass_kernel_spmd

    def edges(name, fill):
        v = np.asarray(inputs[name]).reshape(-1)
        pad = -v.shape[0] % (CHUNK * ROWS)
        v = np.pad(v, (0, pad), constant_values=fill)
        return v.reshape(-1, P, TILES).transpose(1, 0, 2).reshape(P, -1)

    def edge_rows(name, fill):
        return edges(name, fill).reshape(P, -1, TILES).transpose(1, 2, 0).reshape(1, -1)

    attr = np.asarray(inputs["edge_attr3_1x20"])
    rbf = attr.shape[-1]
    attr = attr.reshape(-1, rbf)
    attr = np.pad(attr, ((0, -attr.shape[0] % (CHUNK * ROWS)), (0, 0)))
    attr = attr.reshape(-1, P, TILES, rbf).transpose(3, 0, 2, 1).reshape(rbf, -1)
    row = lambda name: np.asarray(inputs[name]).reshape(1, -1)
    column = lambda name: np.asarray(inputs[name]).reshape(-1, 1)
    whole = lambda name: np.asarray(inputs[name])
    arrays = {
        "src_row": edge_rows("src", 0), "dst_row": edge_rows("dst", NO_NODE),
        "x": whole("x"), "src": edges("src", 0), "dst": edges("dst", NO_NODE), "attr": attr,
        "ew": edges("edge_weight", 0), "cut": edges("edge_weight1", 0),
        "w_in": whole("L0_gnn_W_in"), "w_f1": whole("L0_gnn_W_f1"), "b_f1": column("L0_gnn_b_f1"),
        "w_f2": whole("L0_gnn_W_f2"), "b_f2": row("L0_gnn_b_f2"), "w_o1": whole("L0_gnn_W_o1"),
        "b_o1": column("L0_gnn_b_o1"), "w_o2": whole("L0_gnn_W_o2"), "b_o2": row("L0_gnn_b_o2"),
        "w_gat": whole("L1_gnn_W"), "a_src": row("L1_gnn_a_src"), "a_dst": row("L1_gnn_a_dst"),
        "w_gc": whole("L2_gnn_weight"), "b_gc": row("L2_gnn_bias"),
        "w_0": whole("L3_gnn_W0"), "b_0": row("L3_gnn_b0"), "w_1": whole("L3_gnn_W1"), "b_1": row("L3_gnn_b1"),
        "slope": row("L3_gnn_prelu_w"), "mixing": row("L3_gnn_mixing"),
    }
    arrays = {f"in_{k}": np.ascontiguousarray(v) for k, v in arrays.items()}
    nc = bacc.Bacc("TRN2", target_bir_lowering=False, num_devices=1)
    a = {k[3:]: nc.dram_tensor(k, v.shape, mybir.dt.from_np(v.dtype), kind="ExternalInput").ap()
         for k, v in arrays.items()}
    out = nc.dram_tensor("out", arrays["in_x"].shape, F32, kind="ExternalOutput").ap()
    build_program(nc, a, out)
    result = run_bass_kernel_spmd(nc, [arrays], core_ids=[0])
    return result.results[0]["out"]
```

```python
from contextlib import ExitStack

import numpy as np

import concourse.bass as bass
from concourse import mybir

F32 = mybir.dt.float32
BF16 = mybir.dt.bfloat16
I32 = mybir.dt.int32
ALU = mybir.AluOpType
ACT = mybir.ActivationFunctionType
AX = mybir.AxisListType

P = 128
D = 128
TILES = 8
CHUNK = P * TILES
ROWS = 4
SUMS = 4
NODES_PER_BATCH = 7
EPS = 1e-5
NO_NODE = -1
SLOPE_GAT = 0.01


class Place:

    def __init__(self, i, n, blocks, w=None, general=False):
        self.c = i * ROWS + n
        self.r, self.turn = n % ROWS, i + n // ROWS
        self.k, self.turn2 = n % 2, i * 2 + n // 2
        self.w, self.general = w, general
        self.s = self.c if w is None else self.c * blocks + w
        self.cols = bass.ds(self.c * TILES, TILES)


class Counter:

    def __init__(self, sem, base):
        self.sem, self.base = sem, base


def build_program(nc, a, out):
    N, _ = a["x"].shape
    E_COLS = a["src"].shape[1]
    CHUNKS = E_COLS // TILES
    BLOCKS = -(-N // P)
    FULL = N // P
    REST = N - FULL * P
    NPAD = BLOCKS * P
    RBF = a["attr"].shape[0]
    NJ = BLOCKS // NODES_PER_BATCH
    BJ = NODES_PER_BATCH
    BW = BJ * P
    HALF = BW // 2
    TW = D + 4
    ONE, ZS, ZD = D, D + 1, D + 2
    ACC = NPAD + P
    MIX = a["mixing"].shape[1]
    assert BLOCKS % BJ == 0 and CHUNKS % ROWS == 0

    tables = [nc.dram_tensor(f"table_{n}", [NPAD if n > 1 else ACC, TW if n == 1 else D], F32, kind="Internal").ap()
              for n in range(5)]
    sums_dram = [nc.dram_tensor(f"sums_{q}", [ACC, D], F32, kind="Internal").ap() for q in range(SUMS)]

    with ExitStack() as ctx:
        def sb(name, cols, dt=F32, rows=P):
            return ctx.enter_context(nc.sbuf_tensor(name, [rows, cols], dt))

        def pb(name, cols, dt=F32):
            return ctx.enter_context(nc.psum_tensor(name, [P, cols], dt))

        def sem(name):
            return ctx.enter_context(nc.semaphore(name))

        def sems(prefix, names):
            return {n: sem(f"{prefix}_{n}") for n in names.split()}

        X = sb("X", BLOCKS * D)
        acc = sb("acc", max(ACC, 6 * CHUNK))
        top = sb("top", max(ACC, 6 * CHUNK))
        stage = sb("stage", max(BLOCKS * TW, ACC, 3 * CHUNK))
        den = stage[:, 0:ACC]
        G = [sb(f"G{r}", TILES * TW) for r in range(ROWS)]
        idx = [sb(f"idx{r}", TILES, I32) for r in range(ROWS)]
        dst_i = sb("dst_i", E_COLS, I32)
        dst = sb("dst", E_COLS)
        ew = sb("ew", E_COLS)
        cut = sb("cut", E_COLS)
        srcf = sb("srcf", E_COLS)
        srch = sb("srch", E_COLS, BF16)
        srcl = sb("srcl", E_COLS, BF16)
        iota16 = sb("iota16", P, BF16)
        S = [sb(f"S{k}", CHUNK) for k in range(2)]
        big = [sb(f"big{k}", CHUNK) for k in range(5)]
        dloc = [sb(f"dloc{k}", TILES) for k in range(2)]
        ident = sb("ident", P)
        iota = sb("iota", P)
        ones = sb("ones", P)
        iota_i = sb("iota_i", P, I32)
        first = sb("first", CHUNKS)
        wbase = sb("wbase", BLOCKS)
        flag_i = sb("flag_i", 1, I32)
        W = {n: sb(f"w_{n}", D) for n in ("in", "f2", "o1", "o2", "gat", "gc", "g0", "g1")}
        wf1 = sb("wf1", D, rows=RBF)
        attr = [sb(f"attr{k}", CHUNK, rows=RBF)[:, :] for k in range(2)]
        attr += [acc[0:RBF, q * CHUNK:(q + 1) * CHUNK] for q in (4, 5)]
        bf1 = sb("bf1", 1)
        bo1 = sb("bo1", 1)
        rowb = {n: sb(f"row_{n}", D) for n in ("bf2", "bo2", "asrc", "adst", "gc", "b0", "b1", "slope")}
        vsrc = sb("vsrc", D)
        vdst = sb("vdst", D)
        vcol = sb("vcol", 2)
        mix = sb("mix", 8)
        csum = sb("csum", 1)
        stat = sb("stat", BLOCKS * 6)
        col = {n: sb(f"col_{n}", BLOCKS) for n in
               ("mean", "diff", "var", "std", "rstd", "scale", "bias", "den", "rden", "t0", "t1", "zs", "zd")}
        hist = sb("hist", BLOCKS)
        degrow = top[0:2, :]
        small = {n: [sb(f"sm_{n}{k}", TILES) for k in range(2)] for n in ("zde", "l", "b", "ex")}
        mcol = {n: [sb(f"mc_{n}{k}", 2) for k in range(2)] for n in ("mx", "old", "t", "l", "pair", "zd")}
        tmp = [sb(f"tmp{k}", P) for k in range(5)]
        onesew = [sb(f"onesew{k}", TILES * 2) for k in range(2)]
        viol = sb("viol", 4)
        gmin = sb("gmin", 4)
        half = sb("half", 1)
        msg = [top[:, k * CHUNK:(k + 1) * CHUNK] for k in range(2)]
        nm_sb = sb("nm_sb", D + 4)
        top_old = sb("top_old", P)
        top_diag = sb("top_diag", P)
        decay = [sb(f"decay{k}", P) for k in range(2)]
        w7 = msg[0][:, 0:BW]
        sums_at = [[G[q][:, 0:BW] for q in range(SUMS)], [top[:, (1 + q) * CHUNK:(1 + q) * CHUNK + BW] for q in range(SUMS)]]
        dst_row = [top[:, (2 + r) * CHUNK:(3 + r) * CHUNK].bitcast(I32) for r in range(ROWS)]
        src_row = [acc[:, r * CHUNK:(r + 1) * CHUNK].bitcast(I32) for r in range(ROWS)]
        same = [stage[:, k * CHUNK:(k + 1) * CHUNK] for k in range(2)]
        earlier = stage[:, 2 * CHUNK:3 * CHUNK]
        src_i = top[:, 0:E_COLS].bitcast(I32)
        h_win = [sb(f"h_win{r}", D) for r in range(ROWS)]
        node_id = [sb(f"node_id{k}", 1) for k in range(2)]
        gather_idx = sb("gather_idx", TILES, I32)
        gather_f = sb("gather_f", TILES)
        dup = {n: sb(f"dup_{n}", TILES) for n in ("count", "is", "away", "to")}
        tri = sb("tri", P)
        pidx = sb("pidx", 1)
        pidx_i = sb("pidx_i", 1, I32)
        trash = sb("trash", 1)
        bf2_part = [sb(f"bf2_part{k}", D, BF16) for k in range(3)]
        bf2_rows = sb("bf2_rows", D, BF16)
        ones16 = sb("ones16", P, BF16)
        far = [G[q][:, 0:E_COLS] for q in range(4)]
        parts_i = G[0][:, 0:E_COLS].bitcast(I32)
        score = sb("score", 2 * BJ)
        deg = sb("deg", 2 * BLOCKS)
        degroot = sb("degroot", 2 * BLOCKS)
        dinv = sb("dinv", 2 * BLOCKS)
        positive = sb("positive", BLOCKS)
        lohot = sb("lohot", TILES * P, BF16)
        hihot = sb("hihot", TILES * BLOCKS, BF16)
        zeros = lohot[:, :].bitcast(F32)[:, 0:ACC // 16]
        h7 = big[0][:, 0:BW]
        lhs7 = big[1][:, 0:BW]
        t7 = big[2][:, 0:BW]
        u7 = big[3][:, 0:BW]
        v7 = big[4][:, 0:BW]

        psA = pb("psA", 1024)
        psB = pb("psB", 1024)
        psC = pb("psC", 512)
        psD = pb("psD", 512)
        psE = pb("psE", 512)
        psF = pb("psF", 512)

        loaded = sem("loaded")
        pool_consts = sem("pool_consts")
        dve_link = sem("dve_link")
        x_tail = sem("x_tail")
        pro = sems("pro", "dst first_row vdiag vrow mix_max mix_exp viol viol_all flag gmin gmin_all scores")
        turns = sem("turns")
        idx_in = [sem(f"idx_in{r}") for r in range(ROWS)]
        rows_in = [sem(f"rows_in{r}") for r in range(ROWS)]
        zd_in = [sem(f"zd_in{k}") for k in range(2)]
        table_out = sem("table_out")
        begun = sem("begun")
        acc_ready = sem("acc_ready")
        out_done = sem("out_done")
        norm = "bn stats1 std1 cols1"
        phases = (
            f"{norm} h tr lhs prod rows",
            f"tr turned mm abs relu exp ln lhs prod upd resid {norm} h scored kept",
            f"counts1 deg1 root1 lhs prod upd resid {norm} rows",
            f"counts1 deg1 root1 lhs prod upd biased resid {norm} h tr turned rows",
            "lhs prod upd biased neg prelu h tr turned rows",
            "lhs prod upd biased neg prelu resid")
        node_sems = {name: sem(f"node_{name}") for name in sorted({m.strip("1") for p in phases for m in p.split()})}
        nd, counted = [], dict.fromkeys(node_sems, 0)
        for phase in phases:
            names = {m.strip("1"): 1 if m.endswith("1") else NJ for m in phase.split()}
            nd.append({m: Counter(node_sems[m], counted[m]) for m in names})
            for m, n in names.items():
                counted[m] += n
        l0 = sems("l0", "pre abs relu exp ln ssp wij node_id spread rows rows_kept msg same compared "
                        "away moved to idx summed out_low out gidx_f gidx gathered over")
        rows_at = [sem(f"rows_at{r}") for r in range(ROWS)]
        h_in = [sem(f"h_in{r}") for r in range(ROWS)]
        zeroed = sem("zeroed")
        sums_clear = sem("sums_clear")
        summed = [sem(f"summed{q}") for q in range(SUMS)]
        all_summed = sem("all_summed")
        sums_in = [sem(f"sums_in{k}") for k in range(2)]
        l1 = sems("l1", "hot hist counted dloc onehot diag masked mx st old_row old_col t1 t2 pair top_diag edge toprow zde leak arg0 "
                        "arg decay_arg top_new ex decay weights nm nm_sb tr scaled added")
        lw = {n: sems(f"l{n}", "dloc onehot sums added" + (" ones" if n == 2 else "")) for n in (2, 3, 4)}

        links = Counter(dve_link, 0)
        TABLE_DMAS = [NJ + 1, NJ + 3, 2 * NJ + 3, 3 * NJ + 3, 4 * NJ + 3]
        TURNS = CHUNKS // ROWS

        LOADS = [(t[:, :], what) for t, what in (
            (dst_i, a["dst"]), (src_i, a["src"]), (ew, a["ew"]), (cut, a["cut"]), (W["in"], a["w_in"]), (W["f2"], a["w_f2"]),
            (W["o1"], a["w_o1"]), (W["o2"], a["w_o2"]), (W["gat"], a["w_gat"]), (W["gc"], a["w_gc"]), (W["g0"], a["w_0"]),
            (W["g1"], a["w_1"]), (wf1, a["w_f1"]), (bf1, a["b_f1"]), (bo1, a["b_o1"]))]
        LOADS += [(rowb[n][:, :], what.to_broadcast([P, D])) for n, what in (
            ("bf2", a["b_f2"]), ("bo2", a["b_o2"]), ("asrc", a["a_src"]), ("adst", a["a_dst"]), ("gc", a["b_gc"]), ("b0", a["b_0"]),
            ("b1", a["b_1"]), ("slope", a["slope"]))]
        LOADS += [(mix[:, 0:MIX], a["mixing"].to_broadcast([P, MIX]))]

        def link(ins):
            links.base += 1
            ins.then_inc(dve_link, 1)
            nc.vector.wait_ge(dve_link, links.base)

        def walk(eng, general, over, near, every_chunk, every_step, lags, credit=False,
                 steps=BLOCKS):
            with eng.If(general > 0):
                if credit:
                    eng.sem_inc(over, 1)
                with eng.Fori(0, CHUNKS // ROWS) as i:
                    for r in range(ROWS):
                        st = Place(i, r, BLOCKS, general=True)
                        if every_chunk:
                            eng.wait_ge(over, st.c * steps + 1)
                            if eng is nc.gpsimd:
                                eng.sem_inc(turns, 1)
                            for stage_ in every_chunk:
                                stage_(st)
                        if every_step:
                            with eng.Fori(0, BLOCKS) as w:
                                st = Place(i, r, BLOCKS, w, general=True)
                                eng.wait_ge(over, st.s + 1)
                                for stage_ in every_step:
                                    stage_(st)
                if credit:
                    eng.wait_ge(over, CHUNKS * steps + 1)
            with eng.Else():
                def turn(i, n):
                    for stage_, lag in near:
                        if not isinstance(i, int) or 0 <= n - lag < CHUNKS:
                            stage_(Place(i, n - lag, BLOCKS))
                for n in range(ROWS):
                    turn(0, n)
                with eng.Fori(0, CHUNKS // ROWS - 1) as i:
                    for n in range(ROWS, 2 * ROWS):
                        turn(i, n)
                for n in range(CHUNKS, CHUNKS + lags):
                    turn(0, n)
                if credit and steps > 1:
                    eng.wait_ge(over, CHUNKS)

        def ready(eng, semaphore, st):
            eng.wait_ge(semaphore, st.s + 1)

        def done_before(eng, semaphore, st, depth):
            if not st.general and not (isinstance(st.s, int) and st.s < depth):
                eng.wait_ge(semaphore, st.s + (1 - depth))

        def batches(eng, body):
            body(0)
            with eng.Fori(1, NJ) as j:
                body(j)

        def skewed(eng, first_half, second_half):
            first_half(0)
            first_half(1)
            second_half(0)
            if NJ > 2:
                with eng.Fori(2, NJ) as j:
                    first_half(j)
                    second_half(j - 1)
            second_half(NJ - 1)

        def reached(eng, counter, n):
            eng.wait_ge(counter.sem, n + counter.base)

        def batch_before(eng, counter, j):
            if not (isinstance(j, int) and j == 0):
                reached(eng, counter, j)

        def tiles(ap, n=TILES):
            return ap.rearrange("p (t f) -> p t f", t=n)

        def over_tiles(ap):
            return ap.unsqueeze(1).to_broadcast([P, TILES, ap.shape[1]])

        def over_blocks(ap):
            return ap.unsqueeze(1).to_broadcast([P, BJ, ap.shape[1]])

        def along(ap, n):
            return ap.unsqueeze(2).to_broadcast([P, ap.shape[1], n])

        def slot(st):
            return st.k if st.w is None else 0

        def hot(st):
            return (S[0], S[1], big[3], big[4])[st.r if st.w is None else 0]

        def bank(st):
            return (psD, psE)[slot(st)]

        def indices_ready(eng, n, st):
            eng.wait_ge(idx_in[st.r], 16 * (st.turn + ((n - 1) * TURNS + 1)))

        def rows_ready(eng, n, st):
            eng.wait_ge(rows_in[st.r], 16 * TILES * (st.turn + ((n - 1) * TURNS + 1)))

        def window(eng, st):
            if st.w is not None:
                return st.w * P
            return eng.value_load(dst_i[0:1, bass.ds(st.c * TILES, 1)], min_val=0, max_val=N - 1)

        def turned_in(j):
            banks = (psC, psD) if j % 2 == 0 else (psE, psF)
            return (banks[0], 0, 4 * P), (banks[1], 4 * P, BW - 4 * P)

        def batch(j, width=D):
            return bass.ds(j * (BJ * width), BJ * width)

        block = ctx.enter_context(nc.Block())

        @block.sync
        def _(sp):
            sp.dma_start(tiles(X[:, 0:FULL * D], FULL),
                         a["x"][0:FULL * P, :].rearrange("(b p) f -> p b f", p=P)).then_inc(loaded, 16)
            if REST:
                sp.wait_ge(x_tail, 1)
                sp.dma_start(X[0:REST, FULL * D:BLOCKS * D], a["x"][FULL * P:N, :]).then_inc(loaded, 16)
            for to, what in LOADS:
                sp.dma_start(to, what).then_inc(loaded, 16)

            sp.wait_ge(pro["flag"], 1)
            general = sp.value_load(flag_i[0:1, 0:1], min_val=0, max_val=1)

            def write_table(n):
                def one(j):
                    reached(sp, nd[n]["rows"], j + 1)
                    sp.dma_start(tables[n][bass.ds(j * BW, BW), :].rearrange("(b p) f -> p b f", p=P),
                                 tiles(stage[:, batch(j)], BJ)).then_inc(table_out, 16)
                with sp.Fori(0, NJ) as j:
                    one(j)

            def load_indices(n):
                def stage_(st):
                    if not (isinstance(st.turn, int) and st.turn == 0 and n == 1) and not st.general:
                        sp.wait_ge(rows_in[st.r], 16 * TILES * (st.turn + (n - 1) * TURNS))
                    sp.dma_start(idx[st.r][:, :], a["src"][:, st.cols]).then_inc(idx_in[st.r], 16)
                return stage_

            def load_edges(st):
                done_before(sp, l0["to"], st, ROWS)
                done_before(sp, l0["spread"], st, ROWS)
                done_before(sp, l0["pre"], st, ROWS)
                sp.dma_start(src_row[st.r], a["src_row"][:, bass.ds(st.c * CHUNK, CHUNK)]
                             .to_broadcast([P, CHUNK])).then_inc(rows_at[st.r], 16)
                sp.dma_start(attr[st.r], a["attr"][:, bass.ds(st.c * CHUNK, CHUNK)]).then_inc(rows_at[st.r], 16)
                sp.dma_start(dst_row[st.r], a["dst_row"][:, bass.ds(st.c * CHUNK, CHUNK)]
                             .to_broadcast([P, CHUNK])).then_inc(rows_at[st.r], 16)

            def load_window(st):
                done_before(sp, l0["rows"], st, ROWS)
                sp.sem_inc(turns, 1)
                sp.dma_start(h_win[st.r][:, :], tables[0][bass.ds(window(sp, st), P), :]).then_inc(h_in[st.r], 16)

            def load_zd(st):
                done_before(sp, l1["pair"], st, 2)
                sp.sem_inc(turns, 1)
                k = 0 if st.w is not None else st.k
                sp.dma_start(mcol["zd"][k][:, 0:2], tables[1][bass.ds(window(sp, st), P), ZD:ZD + 2]).then_inc(zd_in[k], 16)

            sp.wait_ge(zeroed, 1)
            for q in range(SUMS):
                sp.dma_start(sums_dram[q].rearrange("(p n) f -> p (n f)", p=P).rearrange("p (k z) -> p k z", k=16),
                             zeros.unsqueeze(1).to_broadcast([P, 16, ACC // 16])).then_inc(sums_clear, 16)
            write_table(0)
            sp.dma_start(tables[0][NPAD:ACC, :], stage[:, 0:D]).then_inc(table_out, 16)
            sp.wait_ge(table_out, 16 * TABLE_DMAS[0])
            walk(sp, general, l0["over"], [(load_edges, 0), (load_window, 0)], [load_edges], [], 0, steps=1)
            sp.wait_ge(all_summed, 1)

            for j in range(NJ):
                if j >= 2:
                    reached(sp, nd[1]["tr"], j - 1)
                for q in range(SUMS):
                    sp.dma_start(tiles(sums_at[j % 2][q], BJ), sums_dram[q][j * BW:(j + 1) * BW, :]
                                 .rearrange("(b p) f -> p b f", p=P)).then_inc(sums_in[j % 2], 16)
            sp.wait_ge(pro["scores"], 1)
            sp.dma_start(tables[1][0:NPAD, :].rearrange("(b p) f -> p b f", p=P),
                         tiles(stage[:, 0:BLOCKS * TW], BLOCKS)).then_inc(table_out, 16)
            sp.dma_start(tables[1][NPAD:ACC, :], stage[:, 0:TW]).then_inc(table_out, 16)
            sp.wait_ge(table_out, 16 * TABLE_DMAS[1])
            walk(sp, general, l1["added"], [(load_indices(1), 0), (load_zd, 0)], [load_indices(1)], [load_zd], 0)
            for n in (2, 3, 4):
                write_table(n)
                walk(sp, general, lw[n]["added"], [(load_indices(n), 0)], [load_indices(n)], [], 0)
            for j in range(NJ):
                reached(sp, nd[5]["resid"], j + 1)
                last = min((j + 1) * BJ, FULL)
                sp.dma_start(out[j * BW:last * P, :].rearrange("(b p) f -> p b f", p=P),
                             tiles(X[:, j * BW:last * D], last - j * BJ)).then_inc(out_done, 16)
            if REST:
                sp.dma_start(out[FULL * P:N, :], X[0:REST, FULL * D:BLOCKS * D]).then_inc(out_done, 16)
            sp.wait_ge(out_done, 16 * (NJ + (REST > 0)))

        @block.gpsimd
        def _(pool):
            pool.memset(ident[:, :], 0.0).then_inc(pool_consts, 1)
            pool.memset(ones[:, :], 1.0).then_inc(pool_consts, 1)
            pool.iota(iota_i[:, :], pattern=[[1, P]], base=0, channel_multiplier=0).then_inc(pool_consts, 1)
            pool.iota(pidx_i[:, :], pattern=[[0, 1]], base=0, channel_multiplier=1).then_inc(pool_consts, 1)
            pool.wait_ge(pool_consts, 4)
            pool.affine_select(out=ident[:, :], in_=ident[:, :], compare_op=ALU.not_equal, fill=1.0, base=0,
                               pattern=[[-1, P]], channel_multiplier=1).then_inc(pool_consts, 1)
            pool.wait_ge(pro["viol"], 1)
            pool.partition_all_reduce(viol[:, 1:2], viol[:, 0:1], P,
                                      bass.bass_isa.ReduceOp.max).then_inc(pro["viol_all"], 1)
            pool.wait_ge(pro["flag"], 1)
            general = pool.value_load(flag_i[0:1, 0:1], min_val=0, max_val=1)

            def gather(n, slot_free):
                width = TW if n == 1 else D

                def stage_(st):
                    if not st.general and not isinstance(st.c, int):
                        pool.wait_ge(slot_free, st.c - (ROWS - 1))
                        pool.sem_inc(turns, 1)
                    indices_ready(pool, n, st)
                    pool.sem_inc(turns, 1)
                    for t in range(TILES):
                        pool.indirect_dma_start(
                            G[st.r][:, t * width:(t + 1) * width], None, tables[n],
                            bass.IndirectOffsetOnAxis(ap=idx[st.r][:, t:t + 1], axis=0)).then_inc(rows_in[st.r], 16)
                return stage_

            def gather_rows(st):
                ready(pool, l0["gidx"], st)
                pool.sem_inc(turns, 1)
                for t in range(TILES):
                    pool.indirect_dma_start(
                        G[st.r][:, t * D:(t + 1) * D], None, tables[0],
                        bass.IndirectOffsetOnAxis(ap=gather_idx[:, t:t + 1], axis=0)).then_inc(l0["gathered"], 16)

            def scatter(st):
                ready(pool, l0["idx"], st)
                pool.sem_inc(turns, 1)
                ready(pool, l0["out"], st)
                pool.sem_inc(turns, 1)
                for t in range(TILES):
                    if not (t < SUMS and (st.general or isinstance(st.c, int) and st.c == 0)):
                        pool.wait_ge(summed[t % SUMS], st.c * (16 * TILES // SUMS) + 16 * (t // SUMS))
                        pool.sem_inc(turns, 1)
                    pool.indirect_dma_start(
                        sums_dram[t % SUMS], bass.IndirectOffsetOnAxis(ap=idx[st.r][:, t:t + 1], axis=0),
                        G[st.r][:, t * D:(t + 1) * D], None, compute_op=ALU.add).then_inc(summed[t % SUMS], 16)

            def chunk_over(st):
                for q in range(SUMS):
                    pool.wait_ge(summed[q], (st.c + 1) * (16 * TILES // SUMS))
                    pool.sem_inc(turns, 1)
                pool.sem_inc(l0["over"], 1)

            pool.wait_ge(table_out, 16 * TABLE_DMAS[0])
            pool.wait_ge(sums_clear, 16 * SUMS)
            walk(pool, general, l0["over"], [(scatter, 2)], [gather_rows, scatter, chunk_over], [], 2, credit=True, steps=1)
            for q in range(SUMS):
                pool.wait_ge(summed[q], CHUNKS * 16 * TILES // SUMS)
            pool.sem_inc(all_summed, 1)

            frees = [None, l1["nm"], lw[2]["sums"], lw[3]["sums"], lw[4]["sums"]]
            overs = [None, l1["added"], lw[2]["added"], lw[3]["added"], lw[4]["added"]]
            for n in range(1, 5):
                if n == 1:
                    pool.wait_ge(pro["gmin"], 1)
                    pool.partition_all_reduce(gmin[:, 1:2], gmin[:, 0:1], P,
                                              bass.bass_isa.ReduceOp.max).then_inc(pro["gmin_all"], 1)
                pool.wait_ge(table_out, 16 * TABLE_DMAS[n])
                pool.wait_ge(acc_ready, n)
                g = gather(n, frees[n])
                walk(pool, general, overs[n], [(g, 0)], [g], [], 0)

        @block.scalar
        def _(act):
            A = nc.scalar

            def normalized(n, to_stage=False):
                def body(j):
                    s = nd[n]
                    if n == 1:
                        for b in range(BJ):
                            ins = A.activation(stage[:, bass.ds(j * (BJ * TW) + b * TW, D)], X[:, bass.ds(j * BW + b * D, D)],
                                               ACT.Relu, bias=col["bias"][:, bass.ds(j * BJ + b, 1)],
                                               scale=col["scale"][:, bass.ds(j * BJ + b, 1)])
                        ins.then_inc(s["h"].sem, 1)
                        return
                    if not to_stage:
                        batch_before(act, s["tr"] if n in (0, 3) else s["rows"], j)
                        if n == 3:
                            batch_before(act, s["rows"], j)
                    for b in range(BJ):
                        at = bass.ds(j * BW + b * D, D)
                        to = stage[:, at] if to_stage else h7[:, b * D:(b + 1) * D]
                        ins = A.activation(to, X[:, at], ACT.Relu,
                                           bias=col["bias"][:, bass.ds(j * BJ + b, 1)],
                                           scale=col["scale"][:, bass.ds(j * BJ + b, 1)])
                    ins.then_inc((s["rows"] if to_stage else s["h"]).sem, 1)
                return body

            def turned_to_lhs(n):
                def body(j):
                    reached(act, nd[n]["tr"], j + 1)
                    batch_before(act, nd[n]["prod"], j)
                    A.copy(lhs7, psA[:, 0:BW]).then_inc(nd[n]["lhs"].sem, 1)
                return body

            def turned_to_acc(n):
                def body(j):
                    reached(act, nd[n]["tr"], j + 1)
                    act.sem_inc(turns, 1)
                    A.copy(acc[:, batch(j)], psA[:, 0:BW]).then_inc(nd[n]["turned"].sem, 1)
                return body

            def acc_to_lhs(n):
                def body(j):
                    batch_before(act, nd[n]["prod"], j)
                    act.sem_inc(turns, 1)
                    A.copy(lhs7, acc[:, batch(j)]).then_inc(nd[n]["lhs"].sem, 1)
                return body

            def sqrt_of(n):
                reached(act, nd[n]["stats"], 1)
                A.activation(col["std"][:, :], col["var"][:, :], ACT.Sqrt).then_inc(nd[n]["std"].sem, 1)
                reached(act, nd[n]["cols"], 1)

            def roots_of_degrees(n):
                reached(act, nd[n]["deg"], 1)
                A.activation(degroot[:, :], deg[:, :], ACT.Sqrt).then_inc(nd[n]["root"].sem, 1)

            act.wait_ge(pro["mix_max"], 1)
            A.activation(mix[:, 3:6], mix[:, 0:3], ACT.Exp, bias=mix[:, 6:7]).then_inc(pro["mix_exp"], 1)
            sqrt_of(0)
            rows_of, lhs_of = normalized(0), turned_to_lhs(0)

            def table_rows_0(j):
                reached(act, nd[0]["prod"], j + 1)
                act.sem_inc(turns, 1)
                A.copy(stage[:, batch(j)], psB[:, 0:BW]).then_inc(nd[0]["rows"].sem, 1)

            rows_of(0)
            lhs_of(0)
            with act.Fori(1, NJ) as j:
                rows_of(j)
                table_rows_0(j - 1)
                lhs_of(j)
            table_rows_0(NJ - 1)
            act.wait_ge(pro["flag"], 1)
            general = act.value_load(flag_i[0:1, 0:1], min_val=0, max_val=1)

            def filter_ssp(st):
                ready(act, l0["pre"], st)
                done_before(act, l0["ssp"], st, 1)
                A.activation(big[2][:, :], psA[:, :], ACT.Abs, bias=bf1[:, 0:1]).then_inc(l0["abs"], 1)
                A.activation(big[0][:, :], psA[:, :], ACT.Relu, bias=bf1[:, 0:1]).then_inc(l0["relu"], 1)
                ready(act, l0["abs"], st)
                A.activation(big[3][:, :], big[2][:, :], ACT.Exp, scale=-1.0).then_inc(l0["exp"], 1)
                ready(act, l0["exp"], st)
                A.activation(big[1][:, :], big[3][:, :], ACT.Ln, scale=0.5, bias=half[:, 0:1]).then_inc(l0["ln"], 1)

            def keep_rows(st):
                ready(act, l0["rows"], st)
                if not isinstance(st.c, int) or st.c >= ROWS:
                    for q in range(SUMS):
                        act.wait_ge(summed[q], (st.c - (ROWS - 1)) * (16 * TILES // SUMS))
                for t in range(TILES):
                    half_bank = (psC, psD)[t // (TILES // 2)]
                    at = t % (TILES // 2) * D
                    ins = A.activation(G[st.r][:, t * D:(t + 1) * D], half_bank[:, at:at + D], ACT.Copy,
                                       scale=cut[:, bass.ds(st.c * TILES + t, 1)])
                ins.then_inc(l0["rows_kept"], 1)

            def rows_scaled(st):
                act.wait_ge(l0["gathered"], 16 * TILES * (st.c + 1))
                for t in range(TILES):
                    ins = A.activation(G[st.r][:, t * D:(t + 1) * D], G[st.r][:, t * D:(t + 1) * D], ACT.Copy,
                                       scale=cut[:, bass.ds(st.c * TILES + t, 1)])
                ins.then_inc(l0["rows_kept"], 1)

            def sums_kept(st):
                ready(act, l0["summed"], st)
                A.copy(G[st.r][:, 0:CHUNK // 2], psE[:, :]).then_inc(l0["out_low"], 1)
                A.copy(G[st.r][:, CHUNK // 2:CHUNK], psF[:, :]).then_inc(l0["out"], 1)

            act.wait_ge(begun, 1)
            act.preload_act_table_set("natural_log_exp_and_others")
            walk(act, general, l0["over"], [(sums_kept, 2), (filter_ssp, 0), (keep_rows, 0)], [rows_scaled, filter_ssp, sums_kept], [], 2,
                 steps=1)

            s = nd[1]

            def sums_to_acc(j):
                reached(act, s["tr"], j + 1)
                for half_bank, at, width in turned_in(j):
                    ins = A.copy(acc[:, j * BW + at:j * BW + at + width], half_bank[:, 0:width])
                ins.then_inc(s["turned"].sem, 1)

            def output_ssp(j):
                reached(act, s["mm"], j + 1)
                batch_before(act, s["lhs"], j)
                ps = tiles(psA[:, :], 2)[:, :, 0:HALF]
                A.activation(tiles(t7, 2), ps, ACT.Abs, bias=bo1[:, 0:1]).then_inc(s["abs"].sem, 1)
                A.activation(tiles(h7, 2), ps, ACT.Relu, bias=bo1[:, 0:1]).then_inc(s["relu"].sem, 1)
                reached(act, s["abs"], j + 1)
                A.activation(u7, t7, ACT.Exp, scale=-1.0).then_inc(s["exp"].sem, 1)
                reached(act, s["exp"], j + 1)
                A.activation(v7, u7, ACT.Ln, scale=0.5, bias=half[:, 0:1]).then_inc(s["ln"].sem, 1)

            for j in range(NJ + 1):
                if j < NJ:
                    sums_to_acc(j)
                if j > 0:
                    output_ssp(j - 1)
            sqrt_of(1)
            batches(act, normalized(1))

            def diagonals(st):
                rows_ready(act, 1, st)
                done_before(act, l1["masked"], st, 1)
                for t in range(TILES):
                    ins = A.activation(big[0][:, t * P:(t + 1) * P], ident[:, :], ACT.Copy,
                                       scale=G[st.r][:, t * TW + ZS:t * TW + ZS + 1])
                ins.then_inc(l1["diag"], 1)

            def onehot_turned(st):
                ready(act, l1["masked"], st)
                done_before(act, l1["edge"], st, 2)
                A.activation(big[1 + slot(st)][:, :], psA[:, :], ACT.Sign).then_inc(l1["st"], 1)

            def exps(st):
                ready(act, l1["arg"], st)
                A.activation(small["ex"][slot(st)][:, :], small["b"][slot(st)][:, :], ACT.Exp).then_inc(l1["ex"], 1)
                ready(act, l1["decay_arg"], st)
                A.activation(decay[slot(st)][:, :], decay[slot(st)][:, :], ACT.Exp).then_inc(l1["decay"], 1)

            def node_sums(st):
                ready(act, l1["nm"], st)
                done_before(act, l1["tr"], st, 1)
                A.copy(nm_sb[:, 0:D + 1], psE[:, 0:D + 1]).then_inc(l1["nm_sb"], 1)

            act.wait_ge(begun, 2)
            act.preload_act_table_set("exp_and_others")
            walk(act, general, l1["added"], [(diagonals, 0), (exps, 1), (onehot_turned, 0), (node_sums, 1)],
                 [], [diagonals, onehot_turned, exps, node_sums], 1)

            roots_of_degrees(2)
            act.wait_ge(acc_ready, 2)
            batches(act, acc_to_lhs(2))
            sqrt_of(2)
            batches(act, normalized(2, to_stage=True))
            act.wait_ge(acc_ready, 3)
            roots_of_degrees(3)
            batches(act, acc_to_lhs(3))
            sqrt_of(3)
            rows_of, acc_of = normalized(3), turned_to_acc(3)
            batches(act, lambda j: (rows_of(j), acc_of(j)))
            act.wait_ge(acc_ready, 4)
            lhs_of, acc_of4 = acc_to_lhs(4), turned_to_acc(4)
            skewed(act, lhs_of, acc_of4)
            act.wait_ge(acc_ready, 5)
            batches(act, acc_to_lhs(5))

        @block.tensor
        def _(pe):
            M = nc.tensor

            def batch_transposes(n, j):
                s = nd[n]
                reached(pe, s["h"], j + 1)
                batch_before(pe, s["lhs"] if n == 0 else s["turned"], j)
                for b in range(BJ):
                    ins = M.transpose(psA[:, b * P:(b + 1) * P], h7[:, b * D:(b + 1) * D], ident[:, :])
                ins.then_inc(s["tr"].sem, 1)

            def batch_products(n, w, j):
                s = nd[n]
                reached(pe, s["lhs"], j + 1)
                batch_before(pe, s["rows"] if n == 0 else s["upd"], j)
                for b in range(BJ):
                    ins = M.matmul(psB[:, b * D:(b + 1) * D], lhs7[:, b * P:(b + 1) * P], w[:, :],
                                   start=True, stop=True)
                ins.then_inc(s["prod"].sem, 1)

            pe.wait_ge(pool_consts, 5)
            pe.wait_ge(pro["dst"], 1)
            M.matmul(psC[:, 0:CHUNKS], ones[0:1, :], dst[0:1, :].rearrange("p (c t) -> p c t", t=TILES)[:, :, 0],
                     start=True, stop=True).then_inc(pro["first_row"], 1)
            pe.wait_ge(pro["vdiag"], 1)
            M.matmul(psD[:, 0:P], ones[:, :], tmp[0][:, :], start=True, stop=True)
            M.matmul(psE[:, 0:P], ones[:, :], tmp[1][:, :], start=True, stop=True).then_inc(pro["vrow"], 1)
            batches(pe, lambda j: (batch_transposes(0, j), batch_products(0, W["in"], j)))
            pe.wait_ge(pro["flag"], 1)
            general = pe.value_load(flag_i[0:1, 0:1], min_val=0, max_val=1)

            def filter_one(st):
                pe.wait_ge(rows_at[st.r], 48 * (st.turn + 1))
                done_before(pe, l0["relu"], st, 1)
                for q in range(2):
                    ins = M.matmul(psA[:, q * 512:(q + 1) * 512], wf1[:, :], attr[st.r][:, q * 512:(q + 1) * 512],
                                   start=True, stop=True)
                ins.then_inc(l0["pre"], 1)

            def window_rows(st):
                ready(pe, l0["spread"], st)
                pe.wait_ge(h_in[st.r], 16 * (st.turn + 1))
                done_before(pe, l0["rows_kept"], st, 1)
                for t in range(TILES):
                    half_bank = (psC, psD)[t // (TILES // 2)]
                    at = t % (TILES // 2) * D
                    ins = M.matmul(half_bank[:, at:at + D], S[st.k][:, t * P:(t + 1) * P], h_win[st.r][:, :],
                                   start=True, stop=True)
                ins.then_inc(l0["rows"], 1)

            def filter_two(st):
                ready(pe, l0["ssp"], st)
                done_before(pe, l0["msg"], st, 1)
                for t in range(TILES):
                    M.matmul(psB[:, t * D:(t + 1) * D], ones16[:, :], bf2_rows[:, :], start=True, stop=False)
                    ins = M.matmul(psB[:, t * D:(t + 1) * D], big[4][:, t * P:(t + 1) * P], W["f2"][:, :],
                                   start=False, stop=True)
                ins.then_inc(l0["wij"], 1)

            def source_counts(st):
                pe.wait_ge(l1["hot"], st.c + 1)
                done_before(pe, l1["counted"], st, 1)
                for t in range(TILES):
                    ins = M.matmul(psB[:, 0:BLOCKS], lohot[:, t * P:(t + 1) * P],
                                   hihot[:, t * BLOCKS:(t + 1) * BLOCKS], start=(t == 0), stop=(t == TILES - 1))
                ins.then_inc(l1["hist"], 1)

            def equal_sources_summed(st):
                ready(pe, l0["same"], st)
                ready(pe, l0["msg"], st)
                done_before(pe, l0["out"], st, 1)
                for t in range(TILES):
                    half_bank = (psE, psF)[t // (TILES // 2)]
                    at = t % (TILES // 2) * D
                    ins = M.matmul(half_bank[:, at:at + D], same[st.k][:, t * P:(t + 1) * P],
                                   msg[st.k][:, t * D:(t + 1) * D], start=True, stop=True)
                ins.then_inc(l0["summed"], 1)

            pe.wait_ge(begun, 1)
            walk(pe, general, l0["over"],
                 [(equal_sources_summed, 2), (filter_one, 0), (filter_two, 1), (window_rows, 0)],
                 [filter_one, filter_two, equal_sources_summed], [], 2, steps=1)

            def table_sums_turned(j):
                pe.wait_ge(sums_in[j % 2], 16 * SUMS * (j // 2 + 1))
                if j >= 2:
                    reached(pe, nd[1]["turned"], j - 1)
                for half_bank, at, width in turned_in(j):
                    for b in range(0, width, P):
                        for q in range(SUMS):
                            ins = M.matmul(half_bank[:, b:b + P], sums_at[j % 2][q][:, at + b:at + b + D], ident[:, :],
                                           start=(q == 0), stop=(q == SUMS - 1))
                ins.then_inc(nd[1]["tr"].sem, 1)

            s = nd[1]

            def output_network(j):
                reached(pe, s["turned"], j + 1)
                batch_before(pe, s["relu"], j)
                for q in range(2):
                    ins = M.matmul(psA[:, q * 512:q * 512 + HALF], W["o1"][:, :],
                                   acc[:, bass.ds(j * BW + q * HALF, HALF)], start=True, stop=True)
                ins.then_inc(s["mm"].sem, 1)

            for j in range(NJ + 2):
                if j < NJ:
                    table_sums_turned(j)
                if 0 <= j - 1 < NJ:
                    output_network(j - 1)
                if j >= 2:
                    batch_products(1, W["o2"], j - 2)

            def masked_scores(st):
                ready(pe, l1["onehot"], st)
                ready(pe, l1["diag"], st)
                done_before(pe, l1["mx"], st, 1)
                for t in range(TILES):
                    ins = M.matmul(psA[:, t * P:(t + 1) * P], hot(st)[:, t * P:(t + 1) * P],
                                   big[0][:, t * P:(t + 1) * P], start=True, stop=True)
                ins.then_inc(l1["masked"], 1)

            def per_edge(st):
                ready(pe, l1["pair"], st)
                ready(pe, l1["st"], st)
                done_before(pe, l1["arg"], st, 1)
                for t in range(TILES):
                    ins = M.matmul(psC[:, 2 * t:2 * t + 2], big[1 + slot(st)][:, t * P:(t + 1) * P],
                                   mcol["pair"][slot(st)][:, 0:2], start=True, stop=True)
                ins.then_inc(l1["edge"], 1)
                ready(pe, l1["top_diag"], st)
                done_before(pe, l1["top_new"], st, 1)
                M.matmul(psD[:, 0:P], ones[:, :], top_diag[:, :], start=True, stop=True).then_inc(l1["toprow"], 1)

            def weighted_rows(st):
                ready(pe, l1["weights"], st)
                done_before(pe, l1["nm_sb"], st, 1)
                for t in range(TILES):
                    ins = M.matmul(psE[:, 0:D + 1], hot(st)[:, t * P:(t + 1) * P],
                                   G[st.r][:, t * TW:t * TW + D + 1], start=(t == 0), stop=(t == TILES - 1))
                ins.then_inc(l1["nm"], 1)

            def sums_turned(st):
                ready(pe, l1["nm_sb"], st)
                done_before(pe, l1["added"], st, 1)
                M.matmul(psF[:, 0:P], nm_sb[:, 0:D], ident[:, :], start=True, stop=True)
                M.matmul(psF[:, P:2 * P], nm_sb[:, D:D + 1].to_broadcast([P, P]), ident[:, :],
                         start=True, stop=True).then_inc(l1["tr"], 1)

            pe.wait_ge(begun, 2)
            walk(pe, general, l1["added"], [(per_edge, 1), (masked_scores, 0), (sums_turned, 2), (weighted_rows, 1),
                                           (source_counts, 0)],
                 [source_counts], [masked_scores, per_edge, weighted_rows, sums_turned], 2)

            def weighted_pass(n):
                s = lw[n]

                def sums(st):
                    ready(pe, s["onehot"], st)
                    rows_ready(pe, n, st)
                    done_before(pe, s["added"], st, 2)
                    if n == 2:
                        ready(pe, s["ones"], st)
                        for t in range(TILES):
                            M.matmul(bank(st)[0:2, P:2 * P], onesew[slot(st)][:, 2 * t:2 * t + 2],
                                     S[slot(st)][:, t * P:(t + 1) * P], start=(t == 0), stop=(t == TILES - 1))
                    for t in range(TILES):
                        ins = M.matmul(bank(st)[:, 0:P], G[st.r][:, t * D:(t + 1) * D],
                                       S[slot(st)][:, t * P:(t + 1) * P], start=(t == 0), stop=(t == TILES - 1))
                    ins.then_inc(s["sums"], 1)

                pe.wait_ge(begun, n + 1)
                walk(pe, general, s["added"], [(sums, 0)], [], [sums], 0)

            pe.wait_ge(acc_ready, 2)
            for b in range(BLOCKS):
                ins = M.transpose(psC[:, b:b + 1], den[0:1, b * P:(b + 1) * P], ident[0:1, 0:1])
            ins.then_inc(nd[2]["counts"].sem, 1)
            batches(pe, lambda j: batch_products(2, W["gat"], j))
            weighted_pass(2)
            pe.wait_ge(acc_ready, 3)
            for b in range(BLOCKS):
                ins = M.transpose(psC[:, 2 * b:2 * b + 2], degrow[0:2, b * P:(b + 1) * P], ident[0:2, 0:2])
            ins.then_inc(nd[3]["counts"].sem, 1)
            batches(pe, lambda j: batch_products(3, W["gc"], j))
            batches(pe, lambda j: batch_transposes(3, j))
            weighted_pass(3)
            pe.wait_ge(acc_ready, 4)
            skewed(pe, lambda j: batch_products(4, W["g0"], j), lambda j: batch_transposes(4, j))
            weighted_pass(4)
            pe.wait_ge(acc_ready, 5)
            batches(pe, lambda j: batch_products(5, W["g1"], j))

        @block.vector
        def _(dve):
            V = nc.vector
            if REST:
                V.memset(X[:, FULL * D:BLOCKS * D], 0.0).then_inc(x_tail, 1)
            V.memset(half[:, :], 0.5)
            V.memset(hist[:, :], 0.0)
            V.memset(zeros, 0.0).then_inc(zeroed, 1)
            dve.wait_ge(loaded, 16 * (len(LOADS) + 1 + (REST > 0)))
            dve.wait_ge(pool_consts, 5)
            link(V.tensor_copy(dst[:, :], dst_i[:, :]))
            dve.sem_inc(pro["dst"], 1)
            V.tensor_tensor_reduce(tmp[2][:, :], W["gat"][:, :], rowb["asrc"][:, :], 1.0, 0.0, ALU.mult, ALU.add,
                                   vcol[:, 0:1])
            link(V.tensor_tensor_reduce(tmp[3][:, :], W["gat"][:, :], rowb["adst"][:, :], 1.0, 0.0, ALU.mult, ALU.add,
                                        vcol[:, 1:2]))
            V.tensor_scalar(tmp[0][:, :], ident[:, :], vcol[:, 0:1], None, ALU.mult)
            V.tensor_scalar(tmp[1][:, :], ident[:, :], vcol[:, 1:2], None, ALU.mult).then_inc(pro["vdiag"], 1)
            link(V.tensor_reduce(mix[:, 7:8], mix[:, 0:3], AX.X, ALU.max))
            link(V.tensor_scalar(mix[:, 6:7], mix[:, 7:8], -1.0, None, ALU.mult))
            dve.sem_inc(pro["mix_max"], 1)
            def block_stats(j):
                for b in range(BJ):
                    ins = V.bn_stats(stat[:, bass.ds(j * (BJ * 6) + b * 6, 6)], X[:, bass.ds(j * BW + b * D, D)])
                return ins

            def norm_columns(n, factor=None):
                q = stat[:, :].rearrange("p (b s) -> p b s", s=6)
                c = {k: v[:, :] for k, v in col.items()}
                link(V.tensor_tensor(c["mean"], q[:, :, 1], q[:, :, 4], ALU.add))
                link(V.tensor_tensor(c["diff"], q[:, :, 1], q[:, :, 4], ALU.subtract))
                link(V.tensor_tensor(c["t0"], c["diff"], c["diff"], ALU.mult))
                link(V.tensor_tensor(c["t1"], q[:, :, 2], q[:, :, 5], ALU.add))
                link(V.tensor_scalar(c["var"], c["t1"], 1.0 / D, EPS, ALU.mult, ALU.add))
                V.scalar_tensor_tensor(out=c["var"], in0=c["t0"], scalar=0.25, in1=c["var"], op0=ALU.mult,
                                       op1=ALU.add).then_inc(nd[n]["stats"].sem, 1)
                reached(dve, nd[n]["std"], 1)
                link(V.reciprocal(c["rstd"], c["std"]))
                if factor is None:
                    link(V.tensor_copy(c["scale"], c["rstd"]))
                else:
                    link(V.tensor_tensor(c["scale"], c["rstd"], factor, ALU.mult))
                V.scalar_tensor_tensor(out=c["bias"], in0=c["mean"], scalar=-0.5, in1=c["scale"], op0=ALU.mult,
                                       op1=ALU.mult).then_inc(nd[n]["cols"].sem, 1)

            def start_pass(n, last, clear=()):
                for name in last.split():
                    reached(dve, nd[n][name], NJ)
                for buffer, value in clear:
                    V.memset(buffer, value)
                links.base += 1
                V.memset(viol[:, 2:3], 0.0).then_inc(dve_link, 1)
                dve.wait_ge(dve_link, links.base)
                dve.sem_inc(begun, 1)

            def local_dst(st, s):
                base = first[:, bass.ds(st.c, 1)] if st.w is None else wbase[:, bass.ds(st.w, 1)]
                V.tensor_scalar(dloc[slot(st)][:, :], dst[:, st.cols], base, None, ALU.subtract).then_inc(s["dloc"], 1)

            def onehot(st, s, reader, to, depth=2):
                ready(dve, s["dloc"], st)
                done_before(dve, reader, st, depth)
                V.tensor_tensor(tiles(to[:, :]), over_tiles(iota[:, :]), along(dloc[slot(st)][:, :], P),
                                ALU.is_equal).then_inc(s["onehot"], 1)

            def add_sums(st, s):
                ready(dve, s["sums"], st)
                done_before(dve, s["added"], st, 1)
                at = bass.ds(window(dve, st), P)
                V.tensor_tensor(acc[:, at], acc[:, at], bank(st)[:, 0:P], ALU.add).then_inc(s["added"], 1)

            with dve.Fori(0, NJ) as j:
                block_stats(j).then_inc(nd[0]["bn"].sem, 1)
            reached(dve, nd[0]["bn"], NJ)
            norm_columns(0)

            link(V.tensor_copy(iota[:, :], iota_i[:, :]))
            V.tensor_copy(iota16[:, :], iota_i[:, :])
            link(V.tensor_copy(srcf[:, :], src_i[:, :]))
            link(V.tensor_copy(pidx[:, :], pidx_i[:, :]))
            V.tensor_scalar(tri[:, :], iota[:, :], pidx[:, 0:1], None, ALU.is_lt)
            V.tensor_scalar(trash[:, :], pidx[:, :], float(NPAD), None, ALU.add)
            V.memset(ones16[:, :], 1.0)
            link(V.tensor_copy(bf2_part[0][:, :], rowb["bf2"][:, :]))
            link(V.tensor_tensor(tmp[2][:, :], rowb["bf2"][:, :], bf2_part[0][:, :], ALU.subtract))
            link(V.tensor_copy(bf2_part[1][:, :], tmp[2][:, :]))
            link(V.tensor_tensor(tmp[3][:, :], tmp[2][:, :], bf2_part[1][:, :], ALU.subtract))
            link(V.tensor_copy(bf2_part[2][:, :], tmp[3][:, :]))
            link(V.tensor_scalar(bf2_rows[:, :], bf2_part[0][:, :], ident[:, 0:1], None, ALU.mult))
            for k in (1, 2):
                link(V.scalar_tensor_tensor(out=bf2_rows[:, :], in0=bf2_part[k][:, :], scalar=ident[:, k:k + 1],
                                            in1=bf2_rows[:, :], op0=ALU.mult, op1=ALU.add))
            link(V.tensor_scalar(parts_i, src_i[:, :], 7, None, ALU.arith_shift_right))
            link(V.tensor_copy(srch[:, :], parts_i))
            link(V.tensor_scalar(far[1], dst[:, :], 0.0, None, ALU.is_ge))
            link(V.scalar_tensor_tensor(out=far[2], in0=srch[:, :], scalar=1.0, in1=far[1], op0=ALU.add, op1=ALU.mult))
            link(V.tensor_scalar(srch[:, :], far[2], -1.0, None, ALU.add))
            link(V.tensor_scalar(parts_i, src_i[:, :], P - 1, None, ALU.bitwise_and))
            link(V.tensor_copy(srcl[:, :], parts_i))
            V.tensor_scalar(wbase[:, :], iota[:, 0:BLOCKS], float(P), None, ALU.mult)
            dve.wait_ge(pro["vrow"], 1)
            V.tensor_copy(vsrc[:, :], psD[:, 0:P])
            V.tensor_copy(vdst[:, :], psE[:, 0:P])
            dve.wait_ge(pro["first_row"], 1)
            link(V.tensor_copy(first[:, :], psC[:, 0:CHUNKS]))
            link(V.tensor_tensor(tiles(far[0], CHUNKS), tiles(dst[:, :], CHUNKS), along(first[:, :], TILES),
                                 ALU.subtract))
            link(V.tensor_scalar(far[1], far[0], float(P - 1), None, ALU.is_gt))
            link(V.tensor_scalar(far[2], dst[:, :], 0.0, None, ALU.is_ge))
            link(V.scalar_tensor_tensor(out=far[3], in0=far[0], scalar=0.0, in1=far[2], op0=ALU.is_lt, op1=ALU.mult))
            link(V.tensor_tensor(far[2], far[3], far[1], ALU.max))
            V.tensor_reduce(viol[:, 0:1], far[2], AX.X, ALU.max).then_inc(pro["viol"], 1)
            dve.wait_ge(pro["mix_exp"], 1)
            link(V.tensor_reduce(mix[:, 7:8], mix[:, 3:6], AX.X, ALU.add))
            link(V.reciprocal(mix[:, 6:7], mix[:, 7:8]))
            link(V.tensor_scalar(mix[:, 0:3], mix[:, 3:6], mix[:, 6:7], None, ALU.mult))
            link(V.tensor_reduce(csum[:, :], mix[:, 0:3], AX.X, ALU.add))
            dve.wait_ge(pro["viol_all"], 1)
            V.tensor_copy(flag_i[:, :], viol[:, 1:2]).then_inc(pro["flag"], 1)

            start_pass(0, "rows")
            general = dve.value_load(flag_i[0:1, 0:1], min_val=0, max_val=1)

            def filter_sum(st):
                ready(dve, l0["relu"], st)
                ready(dve, l0["ln"], st)
                done_before(dve, l0["wij"], st, 1)
                V.tensor_tensor(big[4][:, :], big[0][:, :], big[1][:, :], ALU.add).then_inc(l0["ssp"], 1)

            def spread_window(st):
                V.tensor_tensor(node_id[st.k][:, :], pidx[:, :], first[:, bass.ds(st.c, 1)],
                                ALU.add).then_inc(l0["node_id"], 1)
                dve.wait_ge(rows_at[st.r], 48 * (st.turn + 1))
                done_before(dve, l0["rows"], st, 2)
                ready(dve, l0["node_id"], st)
                V.tensor_scalar(S[st.k][:, :], dst_row[st.r], node_id[st.k][:, 0:1], None,
                                ALU.is_equal).then_inc(l0["spread"], 1)

            def gather_indices(st):
                V.tensor_scalar(gather_f[:, :], dst[:, st.cols], 0.0, None, ALU.max).then_inc(l0["gidx_f"], 1)
                ready(dve, l0["gidx_f"], st)
                V.tensor_copy(gather_idx[:, :], gather_f[:, :]).then_inc(l0["gidx"], 1)

            def same_source(st):
                dve.wait_ge(rows_at[st.r], 48 * (st.turn + 1))
                done_before(dve, l0["summed"], st, 2)
                V.tensor_tensor(tiles(same[st.k]), tiles(src_row[st.r]), along(srcf[:, st.cols], P),
                                ALU.is_equal).then_inc(l0["same"], 1)

            def scatter_indices(st):
                done_before(dve, l0["away"], st, 1)
                for t in range(TILES):
                    at = bass.ds(st.c * TILES + t, 1)
                    ins = V.scalar_tensor_tensor(
                        out=earlier[:, t * P:(t + 1) * P], in0=src_row[st.r][:, t * P:(t + 1) * P],
                        scalar=srcf[:, at], in1=tri[:, :], op0=ALU.is_equal, op1=ALU.mult,
                        accum_out=dup["count"][:, t:t + 1])
                ins.then_inc(l0["compared"], 1)
                ready(dve, l0["compared"], st)
                V.tensor_scalar(dup["is"][:, :], dup["count"][:, :], 0.0, None, ALU.is_gt)
                V.tensor_scalar(dup["away"][:, :], srcf[:, st.cols], trash[:, 0:1], -1.0, ALU.subtract,
                                ALU.mult).then_inc(l0["away"], 1)
                ready(dve, l0["away"], st)
                V.tensor_tensor(dup["to"][:, :], dup["is"][:, :], dup["away"][:, :], ALU.mult).then_inc(l0["moved"], 1)
                ready(dve, l0["moved"], st)
                V.tensor_tensor(dup["is"][:, :], dup["to"][:, :], srcf[:, st.cols], ALU.add).then_inc(l0["to"], 1)
                ready(dve, l0["to"], st)
                if not st.general and not (isinstance(st.c, int) and st.c < ROWS):
                    for q in range(SUMS):
                        dve.wait_ge(summed[q], (st.c - (ROWS - 1)) * (16 * TILES // SUMS))
                V.tensor_copy(idx[st.r][:, :], dup["is"][:, :]).then_inc(l0["idx"], 1)

            def messages(st):
                ready(dve, l0["wij"], st)
                ready(dve, l0["rows_kept"], st)
                done_before(dve, l0["summed"], st, 2)
                V.tensor_tensor(msg[st.k], psB[:, :], G[st.r][:, 0:CHUNK], ALU.mult).then_inc(l0["msg"], 1)

            def weighted_onehot(s, weight):
                def stage_(st):
                    local_dst(st, s)
                    ready(dve, s["dloc"], st)
                    done_before(dve, s["sums"], st, 2)
                    for t in range(TILES):
                        ins = V.tensor_scalar(S[slot(st)][:, t * P:(t + 1) * P], iota[:, :],
                                              dloc[slot(st)][:, t:t + 1], weight[:, bass.ds(st.c * TILES + t, 1)],
                                              ALU.is_equal, ALU.mult)
                    ins.then_inc(s["onehot"], 1)
                return stage_

            walk(dve, general, l0["over"],
                 [(filter_sum, 1), (spread_window, 0), (same_source, 1), (scatter_indices, 1), (messages, 1)],
                 [gather_indices, filter_sum, messages, same_source, scatter_indices], [], 1, steps=1)

            s1 = nd[1]

            def output_ssp_summed(j):
                reached(dve, s1["ln"], j + 1)
                reached(dve, s1["relu"], j + 1)
                batch_before(dve, s1["prod"], j)
                V.tensor_tensor(lhs7, h7, v7, ALU.add).then_inc(s1["lhs"].sem, 1)

            def node_1(j):
                reached(dve, s1["prod"], j + 1)
                V.tensor_tensor(tiles(w7, BJ), tiles(psB[:, 0:BW], BJ), over_blocks(rowb["bo2"][:, :]),
                                ALU.add).then_inc(s1["upd"].sem, 1)
                reached(dve, s1["upd"], j + 1)
                V.tensor_tensor(X[:, batch(j)], X[:, batch(j)], w7, ALU.add).then_inc(s1["resid"].sem, 1)
                reached(dve, s1["resid"], j + 1)
                block_stats(j).then_inc(s1["bn"].sem, 1)
            skewed(dve, output_ssp_summed, node_1)
            dve.sem_inc(acc_ready, 1)
            reached(dve, s1["bn"], NJ)
            norm_columns(1)
            stage_t = stage[:, 0:BLOCKS * TW].rearrange("p (b w) -> p b w", w=TW)
            V.memset(stage_t[:, :, ONE:TW], 1.0)

            def scores(j):
                reached(dve, s1["h"], j + 1)
                batch_before(dve, s1["kept"], j)
                for b in range(BJ):
                    hb = stage[:, bass.ds(j * (BJ * TW) + b * TW, D)]
                    V.scalar_tensor_tensor(out=t7[:, b * D:(b + 1) * D], in0=hb, scalar=1.0, in1=vsrc[:, :],
                                           op0=ALU.mult, op1=ALU.mult, accum_out=score[:, b:b + 1])
                    ins = V.scalar_tensor_tensor(out=u7[:, b * D:(b + 1) * D], in0=hb, scalar=1.0, in1=vdst[:, :],
                                                 op0=ALU.mult, op1=ALU.mult, accum_out=score[:, BJ + b:BJ + b + 1])
                ins.then_inc(s1["scored"].sem, 1)
                reached(dve, s1["scored"], j + 1)
                V.tensor_copy(col["zs"][:, bass.ds(j * BJ, BJ)], score[:, 0:BJ])
                V.tensor_copy(col["zd"][:, bass.ds(j * BJ, BJ)], score[:, BJ:2 * BJ]).then_inc(s1["kept"].sem, 1)
            batches(dve, scores)
            reached(dve, s1["kept"], NJ)
            link(V.tensor_reduce(gmin[:, 2:3], col["zs"][:, :], AX.X, ALU.min))
            V.tensor_scalar(gmin[:, 0:1], gmin[:, 2:3], -1.0, None, ALU.mult).then_inc(pro["gmin"], 1)
            dve.wait_ge(pro["gmin_all"], 1)
            link(V.tensor_scalar(stage_t[:, :, ZS], col["zs"][:, :], gmin[:, 1:2], 1.0, ALU.add, ALU.add))
            link(V.tensor_scalar(stage_t[:, :, ZD], col["zd"][:, :], gmin[:, 1:2], 1.0, ALU.subtract, ALU.subtract))
            dve.sem_inc(pro["scores"], 1)
            V.memset(acc[:, :], 0.0)
            V.memset(top[:, :], -3.0e38)
            dve.wait_ge(table_out, 16 * TABLE_DMAS[1])
            start_pass(1, "kept", [(den, 0.0)])

            def source_hots(st):
                done_before(dve, l1["hist"], st, 1)
                V.tensor_tensor(tiles(lohot[:, :]), over_tiles(iota16[:, :]), along(srcl[:, st.cols], P), ALU.is_equal)
                V.tensor_tensor(tiles(hihot[:, :]), over_tiles(iota16[:, 0:BLOCKS]), along(srch[:, st.cols], BLOCKS),
                                ALU.is_equal).then_inc(l1["hot"], 1)

            def count_sources(st):
                ready(dve, l1["hist"], st)
                done_before(dve, l1["counted"], st, 1)
                V.tensor_tensor(hist[:, :], hist[:, :], psB[:, 0:BLOCKS], ALU.add).then_inc(l1["counted"], 1)
                if st.general:
                    ready(dve, l1["counted"], st)
                    dve.sem_inc(turns, 1)

            def window_onehot(st):
                local_dst(st, l1)
                onehot(st, l1, l1["nm"], hot(st), ROWS)

            def largest(st):
                ready(dve, l1["st"], st)
                V.tensor_reduce(mcol["mx"][slot(st)][:, 0:1], psA[:, :], AX.X, ALU.max).then_inc(l1["mx"], 1)

            held = {}

            def new_maxima(st):
                k = slot(st)
                done_before(dve, l1["top_new"], st, 1)
                at = bass.ds(window(dve, st), P)
                held["window"] = at
                V.tensor_copy(top_old[:, :], top[:, at]).then_inc(l1["old_row"], 1)
                if st.w is None:
                    dve.wait_ge(zd_in[k], 16 * (st.turn2 + 1))
                else:
                    dve.wait_ge(zd_in[0], 16 * (st.s + 1))
                ready(dve, l1["mx"], st)
                V.tensor_tensor(mcol["t"][k][:, 0:1], mcol["mx"][k][:, 0:1], mcol["zd"][k][:, 0:1],
                                ALU.add).then_inc(l1["t1"], 1)
                ready(dve, l1["old_row"], st)
                V.tensor_tensor_reduce(tmp[4][:, :], top_old[:, :], ident[:, :], 1.0, 0.0, ALU.mult, ALU.add,
                                       mcol["old"][k][:, 0:1]).then_inc(l1["old_col"], 1)
                ready(dve, l1["t1"], st)
                V.scalar_tensor_tensor(out=mcol["l"][k][:, 0:1], in0=mcol["t"][k][:, 0:1], scalar=SLOPE_GAT,
                                       in1=mcol["t"][k][:, 0:1], op0=ALU.mult, op1=ALU.max).then_inc(l1["t2"], 1)
                done_before(dve, l1["edge"], st, 2)
                V.tensor_copy(mcol["pair"][k][:, 0:1], mcol["zd"][k][:, 0:1])
                ready(dve, l1["t2"], st)
                ready(dve, l1["old_col"], st)
                V.tensor_tensor(mcol["pair"][k][:, 1:2], mcol["l"][k][:, 0:1], mcol["old"][k][:, 0:1],
                                ALU.max).then_inc(l1["pair"], 1)
                ready(dve, l1["pair"], st)
                done_before(dve, l1["toprow"], st, 1)
                V.tensor_scalar(top_diag[:, :], ident[:, :], mcol["pair"][k][:, 1:2], None,
                                ALU.mult).then_inc(l1["top_diag"], 1)

            def exponents(st):
                k = slot(st)
                e = psC[:, 0:2 * TILES].rearrange("p (t o) -> p t o", o=2)
                ready(dve, l1["edge"], st)
                V.tensor_tensor(small["zde"][k][:, :], tiles(G[st.r][:, :])[:, :, ZS], e[:, :, 0],
                                ALU.add).then_inc(l1["zde"], 1)
                ready(dve, l1["toprow"], st)
                done_before(dve, l1["added"], st, 2)
                V.tensor_tensor(decay[k][:, :], top_old[:, :], psD[:, 0:P], ALU.subtract).then_inc(l1["decay_arg"], 1)
                ready(dve, l1["zde"], st)
                V.scalar_tensor_tensor(out=small["l"][k][:, :], in0=small["zde"][k][:, :], scalar=SLOPE_GAT,
                                       in1=small["zde"][k][:, :], op0=ALU.mult, op1=ALU.max).then_inc(l1["leak"], 1)
                V.tensor_copy(top[:, held["window"]], psD[:, 0:P]).then_inc(l1["top_new"], 1)
                ready(dve, l1["leak"], st)
                V.tensor_tensor(small["zde"][k][:, :], small["l"][k][:, :], e[:, :, 1],
                                ALU.subtract).then_inc(l1["arg0"], 1)
                ready(dve, l1["arg0"], st)
                V.tensor_scalar(small["b"][k][:, :], small["zde"][k][:, :], 0.0, None, ALU.min).then_inc(l1["arg"], 1)

            def weights(st):
                ready(dve, l1["ex"], st)
                V.tensor_tensor(tiles(hot(st)[:, :]), tiles(hot(st)[:, :]),
                                along(small["ex"][slot(st)][:, :], P), ALU.mult).then_inc(l1["weights"], 1)

            def merge(st):
                at = bass.ds(window(dve, st), P)
                ready(dve, l1["decay"], st)
                done_before(dve, l1["added"], st, 1)
                V.tensor_tensor(tmp[0][:, :], acc[:, at], decay[slot(st)][:, :], ALU.mult)
                V.tensor_tensor(tmp[1][:, :], den[:, at], decay[slot(st)][:, :], ALU.mult).then_inc(l1["scaled"], 1)
                ready(dve, l1["scaled"], st)
                ready(dve, l1["tr"], st)
                V.tensor_tensor(acc[:, at], tmp[0][:, :], psF[:, 0:P], ALU.add)
                V.tensor_tensor(den[:, at], tmp[1][:, :], psF[:, P:2 * P], ALU.add).then_inc(l1["added"], 1)

            walk(dve, general, l1["added"],
                 [(new_maxima, 1), (window_onehot, 0), (count_sources, 1), (exponents, 1), (source_hots, 0), (weights, 1),
                  (merge, 2), (largest, 0)],
                 [source_hots, count_sources], [window_onehot, largest, new_maxima, exponents, weights, merge], 2, credit=True)
            dve.wait_ge(l1["counted"], CHUNKS)
            dve.sem_inc(acc_ready, 1)

            def reciprocal_roots(n):
                links.base += 1
                V.memset(viol[:, 3:4], 0.0).then_inc(dve_link, 1)
                dve.wait_ge(dve_link, links.base)
                dve.sem_inc(nd[n]["deg"].sem, 1)
                reached(dve, nd[n]["root"], 1)
                link(V.reciprocal(dinv[:, :], degroot[:, :]))

            link(V.memset(deg[:, :], 1.0))
            link(V.tensor_scalar(deg[:, 0:BLOCKS], hist[:, :], 1.0, None, ALU.max))
            reciprocal_roots(2)
            s2 = nd[2]
            reached(dve, s2["counts"], 1)
            link(V.tensor_scalar(col["den"][:, :], psC[:, 0:BLOCKS], 1e-37, None, ALU.max))
            link(V.reciprocal(col["rden"][:, :], col["den"][:, :]))

            def node_2(j):
                reached(dve, s2["prod"], j + 1)
                V.tensor_tensor(tiles(t7, BJ), tiles(psB[:, 0:BW], BJ),
                                along(col["rden"][:, bass.ds(j * BJ, BJ)], D), ALU.mult).then_inc(s2["upd"].sem, 1)
                reached(dve, s2["upd"], j + 1)
                V.tensor_tensor(X[:, batch(j)], X[:, batch(j)], t7, ALU.add).then_inc(s2["resid"].sem, 1)
                reached(dve, s2["resid"], j + 1)
                block_stats(j).then_inc(s2["bn"].sem, 1)
            batches(dve, node_2)
            reached(dve, s2["bn"], NJ)
            norm_columns(2, dinv[:, 0:BLOCKS])
            reached(dve, s2["rows"], NJ)
            for k in range(2):
                V.memset(onesew[k][:, :], 1.0)
            start_pass(2, "resid bn", [(acc[:, :], 0.0), (degrow, 0.0)])

            def counting_onehot(st):
                s = lw[2]
                local_dst(st, s)
                V.tensor_copy(onesew[slot(st)][:, :].rearrange("p (t o) -> p t o", o=2)[:, :, 1], ew[:, st.cols])\
                    .then_inc(s["ones"], 1)
                onehot(st, s, s["sums"], S[slot(st)])

            def add2(st):
                s = lw[2]
                ready(dve, s["sums"], st)
                done_before(dve, s["added"], st, 1)
                at = bass.ds(window(dve, st), P)
                V.tensor_tensor(degrow[:, at], degrow[:, at], bank(st)[0:2, P:2 * P], ALU.add)
                V.tensor_tensor(acc[:, at], acc[:, at], bank(st)[:, 0:P], ALU.add).then_inc(s["added"], 1)

            def weighted_pass(n):
                s = lw[n]
                hot = weighted_onehot(s, ew)

                def add(st):
                    add_sums(st, s)
                walk(dve, general, s["added"], [(hot, 0), (add, 1)], [], [hot, add], 1, credit=True)
                dve.sem_inc(acc_ready, 1)

            walk(dve, general, lw[2]["added"], [(counting_onehot, 0), (add2, 1)], [], [counting_onehot, add2], 1,
                 credit=True)
            dve.sem_inc(acc_ready, 1)

            s3 = nd[3]
            reached(dve, s3["counts"], 1)
            counts = psC[:, 0:2 * BLOCKS].rearrange("p (b o) -> p b o", o=2)
            V.tensor_scalar(deg[:, 0:BLOCKS], counts[:, :, 0], 1.0, None, ALU.max)
            link(V.tensor_scalar(deg[:, BLOCKS:2 * BLOCKS], counts[:, :, 1], 1.0, None, ALU.add))
            link(V.tensor_scalar(positive[:, :], deg[:, BLOCKS:2 * BLOCKS], 0.0, None, ALU.is_gt))
            link(V.tensor_scalar(deg[:, BLOCKS:2 * BLOCKS], deg[:, BLOCKS:2 * BLOCKS], 1e-30, None, ALU.max))
            reciprocal_roots(3)
            link(V.tensor_tensor(dinv[:, BLOCKS:2 * BLOCKS], dinv[:, BLOCKS:2 * BLOCKS], positive[:, :], ALU.mult))

            def scaled_and_biased(s, j, first_col, bias):
                reached(dve, s["prod"], j + 1)
                V.tensor_tensor(tiles(t7, BJ), tiles(psB[:, 0:BW], BJ),
                                along(dinv[:, bass.ds(j * BJ + first_col, BJ)], D), ALU.mult).then_inc(s["upd"].sem, 1)
                reached(dve, s["upd"], j + 1)
                V.tensor_tensor(tiles(t7, BJ), tiles(t7, BJ), over_blocks(bias[:, :]), ALU.add).then_inc(s["biased"].sem, 1)
                reached(dve, s["biased"], j + 1)

            def node_3(j):
                scaled_and_biased(s3, j, 0, rowb["gc"])
                V.scalar_tensor_tensor(out=X[:, batch(j)], in0=t7, scalar=0.0, in1=X[:, batch(j)], op0=ALU.max,
                                       op1=ALU.add).then_inc(s3["resid"].sem, 1)
                reached(dve, s3["resid"], j + 1)
                block_stats(j).then_inc(s3["bn"].sem, 1)
            batches(dve, node_3)
            reached(dve, s3["bn"], NJ)
            norm_columns(3, dinv[:, BLOCKS:2 * BLOCKS])

            def rows_to_stage(s):
                def body(j):
                    reached(dve, s["h"], j + 1)
                    V.tensor_copy(stage[:, batch(j)], h7).then_inc(s["rows"].sem, 1)
                return body
            batches(dve, rows_to_stage(s3))
            start_pass(3, "resid bn rows turned")
            weighted_pass(3)

            def prelu(s, j, bias):
                scaled_and_biased(s, j, BLOCKS, bias)
                V.scalar_tensor_tensor(out=tiles(u7, BJ), in0=tiles(t7, BJ), scalar=0.0,
                                       in1=over_blocks(rowb["slope"][:, :]), op0=ALU.min,
                                       op1=ALU.mult).then_inc(s["neg"].sem, 1)
                reached(dve, s["neg"], j + 1)
                V.scalar_tensor_tensor(out=t7, in0=t7, scalar=0.0, in1=u7, op0=ALU.max,
                                       op1=ALU.add).then_inc(s["prelu"].sem, 1)
                reached(dve, s["prelu"], j + 1)

            s4 = nd[4]

            def node_4(j):
                prelu(s4, j, rowb["b0"])
                batch_before(dve, s4["tr"], j)
                V.tensor_tensor(tiles(h7, BJ), tiles(t7, BJ), along(dinv[:, bass.ds(j * BJ + BLOCKS, BJ)], D),
                                ALU.mult).then_inc(s4["h"].sem, 1)
                rows_to_stage(s4)(j)
            batches(dve, node_4)
            start_pass(4, "rows turned")
            weighted_pass(4)

            def node_5(j):
                batch_before(dve, nd[5]["resid"], j)
                prelu(nd[5], j, rowb["b1"])
                V.scalar_tensor_tensor(out=X[:, batch(j)], in0=t7, scalar=csum[:, 0:1], in1=X[:, batch(j)],
                                       op0=ALU.mult, op1=ALU.add).then_inc(nd[5]["resid"].sem, 1)
            batches(dve, node_5)


def kernel(**inputs):
    import concourse.bacc as bacc
    from concourse.bass_utils import run_bass_kernel_spmd

    def edges(name, fill):
        v = np.asarray(inputs[name]).reshape(-1)
        pad = -v.shape[0] % (CHUNK * ROWS)
        v = np.pad(v, (0, pad), constant_values=fill)
        return v.reshape(-1, P, TILES).transpose(1, 0, 2).reshape(P, -1)

    def edge_rows(name, fill):
        return edges(name, fill).reshape(P, -1, TILES).transpose(1, 2, 0).reshape(1, -1)

    attr = np.asarray(inputs["edge_attr3_1x20"])
    rbf = attr.shape[-1]
    attr = attr.reshape(-1, rbf)
    attr = np.pad(attr, ((0, -attr.shape[0] % (CHUNK * ROWS)), (0, 0)))
    attr = attr.reshape(-1, P, TILES, rbf).transpose(3, 0, 2, 1).reshape(rbf, -1)
    row = lambda name: np.asarray(inputs[name]).reshape(1, -1)
    column = lambda name: np.asarray(inputs[name]).reshape(-1, 1)
    whole = lambda name: np.asarray(inputs[name])
    arrays = {
        "src_row": edge_rows("src", 0), "dst_row": edge_rows("dst", NO_NODE),
        "x": whole("x"), "src": edges("src", 0), "dst": edges("dst", NO_NODE), "attr": attr,
        "ew": edges("edge_weight", 0), "cut": edges("edge_weight1", 0),
        "w_in": whole("L0_gnn_W_in"), "w_f1": whole("L0_gnn_W_f1"), "b_f1": column("L0_gnn_b_f1"),
        "w_f2": whole("L0_gnn_W_f2"), "b_f2": row("L0_gnn_b_f2"), "w_o1": whole("L0_gnn_W_o1"),
        "b_o1": column("L0_gnn_b_o1"), "w_o2": whole("L0_gnn_W_o2"), "b_o2": row("L0_gnn_b_o2"),
        "w_gat": whole("L1_gnn_W"), "a_src": row("L1_gnn_a_src"), "a_dst": row("L1_gnn_a_dst"),
        "w_gc": whole("L2_gnn_weight"), "b_gc": row("L2_gnn_bias"),
        "w_0": whole("L3_gnn_W0"), "b_0": row("L3_gnn_b0"), "w_1": whole("L3_gnn_W1"), "b_1": row("L3_gnn_b1"),
        "slope": row("L3_gnn_prelu_w"), "mixing": row("L3_gnn_mixing"),
    }
    arrays = {f"in_{k}": np.ascontiguousarray(v) for k, v in arrays.items()}
    nc = bacc.Bacc("TRN2", target_bir_lowering=False, num_devices=1)
    a = {k[3:]: nc.dram_tensor(k, v.shape, mybir.dt.from_np(v.dtype), kind="ExternalInput").ap()
         for k, v in arrays.items()}
    out = nc.dram_tensor("out", arrays["in_x"].shape, F32, kind="ExternalOutput").ap()
    build_program(nc, a, out)
    result = run_bass_kernel_spmd(nc, [arrays], core_ids=[0])
    return result.results[0]["out"]
```
